# Optimizing a Trainium2 kernel written in Bass

```python
import numpy as np
import jax
import jax.numpy as jnp

def _softmax(x, axis=-1):
    return jax.nn.softmax(x, axis=axis)

def _gelu(x):
    return jax.nn.gelu(x, approximate=True)

def _silu(x):
    return jax.nn.silu(x)

def _sigmoid(x):
    return jax.nn.sigmoid(x)

def _layernorm(x, axis=-1, eps=1e-05):
    m = jnp.mean(x, axis=axis, keepdims=True)
    v = jnp.var(x, axis=axis, keepdims=True)
    return (x - m) / jnp.sqrt(v + eps)

def _scatter_add(tgt, idx, src, axis=0):
    return tgt.at[idx].add(src)

def _segment_sum(src, seg, n):
    return jax.ops.segment_sum(src, seg, n)
kernel_name = 'mk_conv_seq_d4_conv_nhwc768_r2_ee526c'

def setup_inputs(seed: int=0):
    np.random.seed(seed)
    _w = jnp.asarray

    def _rec_inputs():
        import jax
        import jax.numpy as jnp
        _gk = jax.random.key(seed)
        x = -4.65e-05 + 0.9999 * jax.random.normal(jax.random.fold_in(_gk, 1), (2, 64, 64, 384), jnp.float32)
        return x
    x = _rec_inputs()

    def _L0_conv_setup():
        import jax, jax.numpy as jnp
        import numpy as np
        NUM_HEADS = 8
        HIDDEN_SIZE = 384
        BLOCK = HIDDEN_SIZE // NUM_HEADS
        FACTOR = 1
        LAMBDA = 0.01
        FRACTION = 1.0
        SCALE = 0.02

        def softshrink(x, lambd):
            return jnp.where(x > lambd, x - lambd, jnp.where(x < -lambd, x + lambd, jnp.zeros_like(x)))
        key = jax.random.key(seed)
        k = jax.random.split(key, 5)
        B, H, W = (4, 64, 64)
        x = jax.random.normal(k[0], (B, H, W, HIDDEN_SIZE), dtype=jnp.float32)
        w1 = SCALE * jax.random.normal(k[1], (2, NUM_HEADS, BLOCK, BLOCK * FACTOR), dtype=jnp.float32)
        b1 = SCALE * jax.random.normal(k[2], (2, NUM_HEADS, BLOCK * FACTOR), dtype=jnp.float32)
        w2 = SCALE * jax.random.normal(k[3], (2, NUM_HEADS, BLOCK * FACTOR, BLOCK), dtype=jnp.float32)
        b2 = SCALE * jax.random.normal(k[4], (2, NUM_HEADS, BLOCK), dtype=jnp.float32)
        return {'x': x, 'w1': w1, 'b1': b1, 'w2': w2, 'b2': b2}
    _L0_conv_all = _L0_conv_setup()
    _L0_conv_in = {k: v for k, v in _L0_conv_all.items() if k in ('w1', 'b1', 'w2', 'b2')}
    del _L0_conv_all

    def _L1_conv_setup():
        import jax, jax.numpy as jnp
        import numpy as np
        B, H, W = (8, 32, 32)
        WIDTH = 384
        NUM_BLOCKS = 8
        MODES = 32
        HSF = 1
        BS = WIDTH // NUM_BLOCKS
        MLP_HIDDEN = 4 * WIDTH

        def _gelu(x):
            return jax.nn.gelu(x, approximate=False)

        def _ln(x, g, b, eps=1e-05):
            mu = jnp.mean(x, axis=-1, keepdims=True)
            var = jnp.var(x, axis=-1, keepdims=True)
            return (x - mu) * jax.lax.rsqrt(var + eps) * g + b

        def afno2d(x, w1, b1, w2, b2):
            b, h, w, c = x.shape
            x_orig = x
            xf = jnp.fft.rfft2(x, axes=(1, 2), norm='ortho')
            hf, wf = (xf.shape[1], xf.shape[2])
            xf = xf.reshape(b, hf, wf, NUM_BLOCKS, BS)
            xk = xf[:, :MODES, :MODES]
            xr, xi = (jnp.real(xk), jnp.imag(xk))
            o1r = _gelu(jnp.einsum('bhwki,kio->bhwko', xr, w1[0]) - jnp.einsum('bhwki,kio->bhwko', xi, w1[1]) + b1[0])
            o1i = _gelu(jnp.einsum('bhwki,kio->bhwko', xi, w1[0]) + jnp.einsum('bhwki,kio->bhwko', xr, w1[1]) + b1[1])
            o2r = jnp.einsum('bhwki,kio->bhwko', o1r, w2[0]) - jnp.einsum('bhwki,kio->bhwko', o1i, w2[1]) + b2[0]
            o2i = jnp.einsum('bhwki,kio->bhwko', o1i, w2[0]) + jnp.einsum('bhwki,kio->bhwko', o1r, w2[1]) + b2[1]
            o2 = jax.lax.complex(o2r, o2i)
            out = jnp.zeros((b, hf, wf, NUM_BLOCKS, BS), jnp.complex64)
            out = out.at[:, :MODES, :MODES].set(o2)
            out = out.reshape(b, hf, wf, c)
            y = jnp.fft.irfft2(out, s=(h, w), axes=(1, 2), norm='ortho').astype(x.dtype)
            return y + x_orig
        key = jax.random.key(seed)
        ks = jax.random.split(key, 8)
        scale = 1.0 / (BS * BS * HSF)
        return {'x': jax.random.normal(ks[0], (B, H, W, WIDTH), jnp.float32), 'ln1_g': jnp.ones((WIDTH,), jnp.float32), 'ln1_b': jnp.zeros((WIDTH,), jnp.float32), 'ln2_g': jnp.ones((WIDTH,), jnp.float32), 'ln2_b': jnp.zeros((WIDTH,), jnp.float32), 'w1': scale * jax.random.uniform(ks[1], (2, NUM_BLOCKS, BS, BS * HSF), jnp.float32), 'b1': scale * jax.random.uniform(ks[2], (2, NUM_BLOCKS, BS * HSF), jnp.float32), 'w2': scale * jax.random.uniform(ks[3], (2, NUM_BLOCKS, BS * HSF, BS), jnp.float32), 'b2': scale * jax.random.uniform(ks[4], (2, NUM_BLOCKS, BS), jnp.float32), 'mlp_w1': 0.02 * jax.random.normal(ks[5], (WIDTH, MLP_HIDDEN), jnp.float32), 'mlp_b1': jnp.zeros((MLP_HIDDEN,), jnp.float32), 'mlp_w2': 0.02 * jax.random.normal(ks[6], (MLP_HIDDEN, WIDTH), jnp.float32), 'mlp_b2': jnp.zeros((WIDTH,), jnp.float32)}
    _L1_conv_all = _L1_conv_setup()
    _L1_conv_in = {k: v for k, v in _L1_conv_all.items() if k in ('ln1_g', 'ln1_b', 'ln2_g', 'ln2_b', 'w1', 'b1', 'w2', 'b2', 'mlp_w1', 'mlp_b1', 'mlp_w2', 'mlp_b2')}
    del _L1_conv_all

    def _L2_conv_setup():
        import jax, jax.numpy as jnp
        import numpy as np
        from jax import lax
        NB = 8
        THRESH = 0.01

        def _clinear(z, wr, wi, bias):
            zr, zi = (z.real, z.imag)
            yr = jnp.einsum('...i,oi->...o', zr, wr) - jnp.einsum('...i,oi->...o', zi, wi)
            yi = jnp.einsum('...i,oi->...o', zr, wi) + jnp.einsum('...i,oi->...o', zi, wr)
            y = lax.complex(yr, yi)
            return y + lax.complex(bias[:, 0], bias[:, 1])

        def _softshrink(v, t):
            return jnp.where(v > t, v - t, jnp.where(v < -t, v + t, jnp.zeros_like(v)))
        key = jax.random.key(seed)
        ks = jax.random.split(key, 7)
        B, H, W, D = (4, 64, 64, 384)
        bs = D // NB
        hid = bs
        scale = np.sqrt(0.5).astype(np.float32)
        kaiming = 1.0 / np.sqrt(bs)
        x = jax.random.normal(ks[0], (B, H, W, D), dtype=jnp.float32)
        w1r = jax.random.uniform(ks[1], (hid, bs), jnp.float32, -kaiming, kaiming) * scale
        w1i = jax.random.uniform(ks[2], (hid, bs), jnp.float32, -kaiming, kaiming) * scale
        b1 = jax.random.normal(ks[3], (hid, 2), dtype=jnp.float32) * 0.02
        kaiming2 = 1.0 / np.sqrt(hid)
        w2r = jax.random.uniform(ks[4], (bs, hid), jnp.float32, -kaiming2, kaiming2) * scale
        w2i = jax.random.uniform(ks[5], (bs, hid), jnp.float32, -kaiming2, kaiming2) * scale
        b2 = jax.random.normal(ks[6], (bs, 2), dtype=jnp.float32) * 0.02
        return {'x': x, 'w1r': w1r, 'w1i': w1i, 'b1': b1, 'w2r': w2r, 'w2i': w2i, 'b2': b2}
    _L2_conv_all = _L2_conv_setup()
    _L2_conv_in = {k: v for k, v in _L2_conv_all.items() if k in ('w1r', 'w1i', 'b1', 'w2r', 'w2i', 'b2')}
    del _L2_conv_all

    def _L3_conv_setup():
        import jax, jax.numpy as jnp
        import numpy as np
        SPARSITY_THRESHOLD = 0.01
        HARD_THRESH_FRAC = 1.0

        def softshrink(x, lam):
            return jnp.where(x > lam, x - lam, jnp.where(x < -lam, x + lam, jnp.zeros_like(x)))

        def compl_mul_add_act(a, b, c):
            tmp = jnp.einsum('bxykis,kiot->stbxyko', a, b)
            real = tmp[0, 0] - tmp[1, 1]
            imag = tmp[1, 0] + tmp[0, 1]
            return jnp.stack([real, imag], axis=-1) + c
        key = jax.random.key(seed)
        k = jax.random.split(key, 5)
        B, H, W, C = (1, 128, 128, 384)
        nb, bs, factor = (8, 48, 1)
        scale = 0.02
        return {'x': jax.random.normal(k[0], (B, H, W, C), dtype=jnp.float32), 'w1': scale * jax.random.normal(k[1], (nb, bs, bs * factor, 2), dtype=jnp.float32), 'b1': scale * jax.random.normal(k[2], (nb, bs * factor, 2), dtype=jnp.float32), 'w2': scale * jax.random.normal(k[3], (nb, bs * factor, bs, 2), dtype=jnp.float32), 'b2': scale * jax.random.normal(k[4], (nb, bs, 2), dtype=jnp.float32)}
    _L3_conv_all = _L3_conv_setup()
    _L3_conv_in = {k: v for k, v in _L3_conv_all.items() if k in ('w1', 'b1', 'w2', 'b2')}
    del _L3_conv_all
    return {'x': x, 'L0_conv_w1': _L0_conv_in['w1'], 'L0_conv_b1': _L0_conv_in['b1'], 'L0_conv_w2': _L0_conv_in['w2'], 'L0_conv_b2': _L0_conv_in['b2'], 'L1_conv_ln1_g': _L1_conv_in['ln1_g'], 'L1_conv_ln1_b': _L1_conv_in['ln1_b'], 'L1_conv_ln2_g': _L1_conv_in['ln2_g'], 'L1_conv_ln2_b': _L1_conv_in['ln2_b'], 'L1_conv_w1': _L1_conv_in['w1'], 'L1_conv_b1': _L1_conv_in['b1'], 'L1_conv_w2': _L1_conv_in['w2'], 'L1_conv_b2': _L1_conv_in['b2'], 'L1_conv_mlp_w1': _L1_conv_in['mlp_w1'], 'L1_conv_mlp_b1': _L1_conv_in['mlp_b1'], 'L1_conv_mlp_w2': _L1_conv_in['mlp_w2'], 'L1_conv_mlp_b2': _L1_conv_in['mlp_b2'], 'L2_conv_w1r': _L2_conv_in['w1r'], 'L2_conv_w1i': _L2_conv_in['w1i'], 'L2_conv_b1': _L2_conv_in['b1'], 'L2_conv_w2r': _L2_conv_in['w2r'], 'L2_conv_w2i': _L2_conv_in['w2i'], 'L2_conv_b2': _L2_conv_in['b2'], 'L3_conv_w1': _L3_conv_in['w1'], 'L3_conv_b1': _L3_conv_in['b1'], 'L3_conv_w2': _L3_conv_in['w2'], 'L3_conv_b2': _L3_conv_in['b2']}

def reference(x, L0_conv_w1, L0_conv_b1, L0_conv_w2, L0_conv_b2, L1_conv_ln1_g, L1_conv_ln1_b, L1_conv_ln2_g, L1_conv_ln2_b, L1_conv_w1, L1_conv_b1, L1_conv_w2, L1_conv_b2, L1_conv_mlp_w1, L1_conv_mlp_b1, L1_conv_mlp_w2, L1_conv_mlp_b2, L2_conv_w1r, L2_conv_w1i, L2_conv_b1, L2_conv_w2r, L2_conv_w2i, L2_conv_b2, L3_conv_w1, L3_conv_b1, L3_conv_w2, L3_conv_b2):
    import jax
    import jax.numpy as jnp

    def _L0_conv_ref(x, w1, b1, w2, b2):
        import jax, jax.numpy as jnp
        import numpy as np
        NUM_HEADS = 8
        HIDDEN_SIZE = 384
        BLOCK = HIDDEN_SIZE // NUM_HEADS
        FACTOR = 1
        LAMBDA = 0.01
        FRACTION = 1.0
        SCALE = 0.02

        def softshrink(x, lambd):
            return jnp.where(x > lambd, x - lambd, jnp.where(x < -lambd, x + lambd, jnp.zeros_like(x)))
        bias = x
        dtype = x.dtype
        xf32 = x.astype(jnp.float32)
        B, H, W, C = x.shape
        xs = jnp.fft.rfft2(xf32, axes=(1, 2))
        Wm = W // 2 + 1
        xs = xs.reshape(B, H, Wm, NUM_HEADS, BLOCK)
        total_modes = H // 2 + 1
        kept = int(total_modes * FRACTION)
        lo, hi = (total_modes - kept, min(total_modes + kept, H))
        wk = min(kept, Wm)
        xr = jnp.real(xs[:, lo:hi, :wk])
        xi = jnp.imag(xs[:, lo:hi, :wk])
        o1r = jax.nn.relu(jnp.einsum('bxyhi,hio->bxyho', xr, w1[0]) - jnp.einsum('bxyhi,hio->bxyho', xi, w1[1]) + b1[0])
        o1i = jax.nn.relu(jnp.einsum('bxyhi,hio->bxyho', xi, w1[0]) + jnp.einsum('bxyhi,hio->bxyho', xr, w1[1]) + b1[1])
        o2r = jnp.einsum('bxyho,hoi->bxyhi', o1r, w2[0]) - jnp.einsum('bxyho,hoi->bxyhi', o1i, w2[1]) + b2[0]
        o2i = jnp.einsum('bxyho,hoi->bxyhi', o1i, w2[0]) + jnp.einsum('bxyho,hoi->bxyhi', o1r, w2[1]) + b2[1]
        zr = jnp.zeros((B, H, Wm, NUM_HEADS, BLOCK), dtype=jnp.float32).at[:, lo:hi, :wk].set(o2r)
        zi = jnp.zeros((B, H, Wm, NUM_HEADS, BLOCK), dtype=jnp.float32).at[:, lo:hi, :wk].set(o2i)
        out_c = softshrink(zr, LAMBDA) + 1j * softshrink(zi, LAMBDA)
        out_c = out_c.reshape(B, H, Wm, C)
        out = jnp.fft.irfft2(out_c, s=(H, W), axes=(1, 2))
        return out.astype(dtype) + bias

    def _L1_conv_ref(x, ln1_g, ln1_b, ln2_g, ln2_b, w1, b1, w2, b2, mlp_w1, mlp_b1, mlp_w2, mlp_b2):
        import jax, jax.numpy as jnp
        import numpy as np
        B, H, W = (8, 32, 32)
        WIDTH = 384
        NUM_BLOCKS = 8
        MODES = 32
        HSF = 1
        BS = WIDTH // NUM_BLOCKS
        MLP_HIDDEN = 4 * WIDTH

        def _gelu(x):
            return jax.nn.gelu(x, approximate=False)

        def _ln(x, g, b, eps=1e-05):
            mu = jnp.mean(x, axis=-1, keepdims=True)
            var = jnp.var(x, axis=-1, keepdims=True)
            return (x - mu) * jax.lax.rsqrt(var + eps) * g + b

        def afno2d(x, w1, b1, w2, b2):
            b, h, w, c = x.shape
            x_orig = x
            xf = jnp.fft.rfft2(x, axes=(1, 2), norm='ortho')
            hf, wf = (xf.shape[1], xf.shape[2])
            xf = xf.reshape(b, hf, wf, NUM_BLOCKS, BS)
            xk = xf[:, :MODES, :MODES]
            xr, xi = (jnp.real(xk), jnp.imag(xk))
            o1r = _gelu(jnp.einsum('bhwki,kio->bhwko', xr, w1[0]) - jnp.einsum('bhwki,kio->bhwko', xi, w1[1]) + b1[0])
            o1i = _gelu(jnp.einsum('bhwki,kio->bhwko', xi, w1[0]) + jnp.einsum('bhwki,kio->bhwko', xr, w1[1]) + b1[1])
            o2r = jnp.einsum('bhwki,kio->bhwko', o1r, w2[0]) - jnp.einsum('bhwki,kio->bhwko', o1i, w2[1]) + b2[0]
            o2i = jnp.einsum('bhwki,kio->bhwko', o1i, w2[0]) + jnp.einsum('bhwki,kio->bhwko', o1r, w2[1]) + b2[1]
            o2 = jax.lax.complex(o2r, o2i)
            out = jnp.zeros((b, hf, wf, NUM_BLOCKS, BS), jnp.complex64)
            out = out.at[:, :MODES, :MODES].set(o2)
            out = out.reshape(b, hf, wf, c)
            y = jnp.fft.irfft2(out, s=(h, w), axes=(1, 2), norm='ortho').astype(x.dtype)
            return y + x_orig
        residual = x
        h = _ln(x, ln1_g, ln1_b)
        h = afno2d(h, w1, b1, w2, b2)
        h = h + residual
        residual = h
        m = _ln(h, ln2_g, ln2_b)
        m = _gelu(m @ mlp_w1 + mlp_b1) @ mlp_w2 + mlp_b2
        return m + residual

    def _L2_conv_ref(x, w1r, w1i, b1, w2r, w2i, b2):
        import jax, jax.numpy as jnp
        import numpy as np
        from jax import lax
        NB = 8
        THRESH = 0.01

        def _clinear(z, wr, wi, bias):
            zr, zi = (z.real, z.imag)
            yr = jnp.einsum('...i,oi->...o', zr, wr) - jnp.einsum('...i,oi->...o', zi, wi)
            yi = jnp.einsum('...i,oi->...o', zr, wi) + jnp.einsum('...i,oi->...o', zi, wr)
            y = lax.complex(yr, yi)
            return y + lax.complex(bias[:, 0], bias[:, 1])

        def _softshrink(v, t):
            return jnp.where(v > t, v - t, jnp.where(v < -t, v + t, jnp.zeros_like(v)))
        B, H, W, D = x.shape
        bs = D // NB
        bias = x
        xf = jnp.fft.rfftn(x, s=(H, W), axes=(1, 2), norm='ortho')
        Fw = xf.shape[2]
        xb = xf.reshape(B, H, Fw, NB, bs)
        h = _clinear(xb, w1r, w1i, b1)
        h = lax.complex(jax.nn.relu(h.real), jax.nn.relu(h.imag))
        y = _clinear(h, w2r, w2i, b2)
        y = y.reshape(B, H, Fw, D)
        y = lax.complex(_softshrink(y.real, THRESH), _softshrink(y.imag, THRESH))
        out = jnp.fft.irfftn(y, s=(H, W), axes=(1, 2), norm='ortho')
        return out + bias

    def _L3_conv_ref(x, w1, b1, w2, b2):
        import jax, jax.numpy as jnp
        import numpy as np
        SPARSITY_THRESHOLD = 0.01
        HARD_THRESH_FRAC = 1.0

        def softshrink(x, lam):
            return jnp.where(x > lam, x - lam, jnp.where(x < -lam, x + lam, jnp.zeros_like(x)))

        def compl_mul_add_act(a, b, c):
            tmp = jnp.einsum('bxykis,kiot->stbxyko', a, b)
            real = tmp[0, 0] - tmp[1, 1]
            imag = tmp[1, 0] + tmp[0, 1]
            return jnp.stack([real, imag], axis=-1) + c
        bias = x
        dtype = x.dtype
        B, H, W, C = x.shape
        nb, bs = (w1.shape[0], w1.shape[1])
        total_modes = H // 2 + 1
        kept_modes = int(total_modes * HARD_THRESH_FRAC)
        lo = total_modes - kept_modes
        hi = min(total_modes + kept_modes, H)
        xf = jnp.fft.rfft2(x.astype(jnp.float32), axes=(1, 2), norm='ortho')
        xf = xf.reshape(B, H, W // 2 + 1, nb, bs)
        xs = jnp.stack([xf.real, xf.imag], axis=-1)
        sub = xs[:, lo:hi, :kept_modes]
        o1 = jax.nn.relu(compl_mul_add_act(sub, w1, b1))
        o2 = jnp.zeros_like(xs).at[:, lo:hi, :kept_modes].set(compl_mul_add_act(o1, w2, b2))
        o2 = softshrink(o2, SPARSITY_THRESHOLD)
        xc = (o2[..., 0] + 1j * o2[..., 1]).reshape(B, H, W // 2 + 1, C)
        out = jnp.fft.irfft2(xc, s=(H, W), axes=(1, 2), norm='ortho').astype(dtype)
        return out + bias

    def _gn(v, G=32, eps=1e-05):
        B_, H_, W_, C_ = v.shape
        g = v.reshape(B_, H_, W_, G, C_ // G)
        m = jnp.mean(g, axis=(1, 2, 4), keepdims=True)
        s = jnp.var(g, axis=(1, 2, 4), keepdims=True)
        return ((g - m) / jnp.sqrt(s + eps)).reshape(v.shape)

    def _ln_c(v, eps=1e-06):
        m = jnp.mean(v, axis=-1, keepdims=True)
        s = jnp.var(v, axis=-1, keepdims=True)
        return (v - m) / jnp.sqrt(s + eps)

    def _ln_t(v, eps=1e-05):
        m = jnp.mean(v, axis=-1, keepdims=True)
        s = jnp.var(v, axis=-1, keepdims=True)
        return (v - m) / jnp.sqrt(s + eps)

    def _to_tokens(v):
        B_, H_, W_, C_ = v.shape
        return v.reshape(B_, H_ * W_, C_)

    def _from_tokens(t, like):
        return t.reshape(like.shape)
    x = _L0_conv_ref(x, L0_conv_w1, L0_conv_b1, L0_conv_w2, L0_conv_b2)
    x = _L1_conv_ref(x, L1_conv_ln1_g, L1_conv_ln1_b, L1_conv_ln2_g, L1_conv_ln2_b, L1_conv_w1, L1_conv_b1, L1_conv_w2, L1_conv_b2, L1_conv_mlp_w1, L1_conv_mlp_b1, L1_conv_mlp_w2, L1_conv_mlp_b2)
    x = _L2_conv_ref(x, L2_conv_w1r, L2_conv_w1i, L2_conv_b1, L2_conv_w2r, L2_conv_w2i, L2_conv_b2)
    x = _L3_conv_ref(x, L3_conv_w1, L3_conv_b1, L3_conv_w2, L3_conv_b2)
    return x

_drawn_inputs = setup_inputs


def setup_inputs(seed=0):
    import zlib

    import numpy as np

    out = dict(_drawn_inputs(seed))
    spreads = {'L1_conv_ln1_g': (1.0, 0.2),
     'L1_conv_ln1_b': (0.0, 0.1),
     'L1_conv_ln2_g': (1.0, 0.6),
     'L1_conv_ln2_b': (0.0, 0.8),
     'L1_conv_mlp_b1': (0.0, 0.374),
     'L1_conv_mlp_b2': (0.0, 0.1)}
    factors = {'L0_conv_b1': 200.0,
     'L0_conv_b2': 64.0,
     'L1_conv_w1': 200.0,
     'L1_conv_b1': 200.0,
     'L1_conv_w2': 200.0,
     'L1_conv_b2': 200.0,
     'L2_conv_b1': 8.0,
     'L2_conv_b2': 4.374,
     'L3_conv_w1': 3.059,
     'L3_conv_b1': 32.269,
     'L3_conv_b2': 4.873}
    for name, (base, spread) in spreads.items():
        noise = np.random.default_rng([zlib.crc32(name.encode()), seed]).standard_normal(out[name].shape)
        drawn = base * np.exp(spread * noise) if base else spread * noise
        out[name] = jnp.asarray(drawn.astype(out[name].dtype))
    for name, factor in factors.items():
        out[name] = (out[name] * factor).astype(out[name].dtype)
    return out
```

```python
from contextlib import ExitStack

import concourse.bass as bass
from concourse import mybir

ALU = mybir.AluOpType
ACT = mybir.ActivationFunctionType
F32 = mybir.dt.float32

P = 128
BATCH, SIDE, CHANNELS = 2, 64, 384
BLOCKS, BLOCK = 8, 48
PAIR = 2 * BLOCK
PAIRS = CHANNELS // PAIR
ROWPAIRS = SIDE * SIDE // P
CHUNK = 4
CHUNKS = ROWPAIRS // CHUNK
HALF = SIDE // 2
HIDDEN = 4 * CHANNELS
KC, HC = CHANNELS // P, HIDDEN // P
TOKENS = 4 * P
TILES = BATCH * SIDE * SIDE // TOKENS
LAMBDA = 0.01
ONE_ROW = BLOCK
ONE_GELU = 8.0
LN_EPS = 1e-5

(C_D1, C_ID, C_D2, C_D2A, C_D2B, C_D5, C_D5A, C_D5B, C_D6) = [P * n for n in range(9)]
C_D5P, C_D5P0, C_SIGN = 9 * P, 11 * P, 13 * P
C_COLS = 13 * P + 3
W_COLS = P + PAIR + 1


class Layer:

    def __init__(self, index, kh, forward, inverse, act, shrink, norm, chain_base):
        self.index, self.kh = index, kh
        self.forward, self.inverse = forward, inverse
        self.act, self.shrink, self.norm = act, shrink, norm
        if kh == SIDE:
            self.groups = [(0, 1, [(0, C_D2A), (0, C_D2B)], 2,
                            [(0, C_D5A, P, 0, True, False), (1, C_D5B, P, 0, False, True)])]
            for s in range(1, HALF, 4):
                n = min(4, HALF - s)
                self.groups.append((s, n, [(j, C_D2) for j in range(n)], n,
                                    [(j, C_D5, P, j * P, True, True) for j in range(n)]))
        else:
            self.groups = []
            for s in range(0, HALF, 4):
                modes = [(j, C_D2A if s + j == 0 else C_D2) for j in range(4)]
                items = [(j, C_D5P0 if s + j == 0 else C_D5P, 2 * P, 2 * j * P, True, True) for j in range(2)]
                self.groups.append((s, 4, modes, 2, items))
        self.units = index * 2 * PAIRS
        self.chain = chain_base
        self.n = len(self.groups)


def iterate(engine, count, body, peel_first):
    if peel_first:
        body(0, False)
    with engine.Fori(1 if peel_first else 0, count - 1) as i:
        body(i, False)
    body(count - 1, True)


def wait_past(engine, semaphore, value):
    if not isinstance(value, int) or value > 0:
        engine.wait_ge(semaphore, value)


def make_layers():
    layers, base = [], 0
    for index, (kh, fwd, inv, act, shrink, norm) in enumerate([
            (SIDE, 1.0, 1.0 / (SIDE * SIDE), ACT.Relu, True, False),
            (HALF, 1.0 / SIDE, 1.0 / SIDE, ACT.Gelu, False, True),
            (SIDE, 1.0 / SIDE, 1.0 / SIDE, ACT.Relu, True, False),
            (SIDE, 1.0 / SIDE, 1.0 / SIDE, ACT.Relu, True, False)]):
        layers.append(Layer(index, kh, fwd, inv, act, shrink, norm, base))
        base += 2 * PAIRS * layers[-1].n
    return layers


def build(nc, x, consts, spectral, ln1, cols, w1, w2, b2, out):
    layers = make_layers()
    with ExitStack() as ctx:
        def sb(name, shape):
            return ctx.enter_context(nc.sbuf_tensor(name, shape, F32))

        def sem(name):
            return ctx.enter_context(nc.semaphore(name))

        after = [nc.dram_tensor(f"after_{n}", (BATCH, SIDE * SIDE, CHANNELS), F32).ap() for n in range(4)]
        layer_in = [x, after[0], after[2], after[3]]
        layer_out = [after[0], after[1], after[3], out]

        UNIT = ROWPAIRS * PAIR
        xs = sb("xs", [P, 2, UNIT])
        xn = sb("xn", [P, 2, UNIT])
        res = sb("res", [P, 2, UNIT])
        y = sb("y", [P, HALF, 2, SIDE])
        z = sb("z", [P, 2, 4 * PAIR + 16])
        zf = sb("zf", [P, 2, 2, 4 * SIDE])
        h = sb("h", [P, 2, 2, 4 * SIDE])
        clamp = sb("clamp", [P, 2, 4 * PAIR])
        u = sb("u", [P, 2, 4, PAIR])
        v = sb("v", [P, SIDE, 2, HALF])
        vt = sb("vt", [P, 2, CHUNK * PAIR])
        wstage = sb("wstage", [P, 2, W_COLS])
        w = sb("w", [P, 2, W_COLS])
        const = sb("const", [P, C_COLS])
        lnrow = sb("lnrow", [P, 2, CHANNELS])
        b2row = sb("b2row", [P, CHANNELS])
        colp = sb("colp", [P, HC + 2 * KC])
        w1s = sb("w1s", [P, KC, HIDDEN])
        w2s = sb("w2s", [P, HC, CHANNELS])
        stat = sb("stat", [P, 2, 4, 6])
        mv = sb("mv", [P, BATCH * ROWPAIRS, 2])
        rstd = sb("rstd", [P, BATCH * ROWPAIRS])
        mv2 = sb("mv2", [P, 2, 4, 2])
        rstd2 = sb("rstd2", [P, 2, 4])
        power = sb("power", [P, BATCH * ROWPAIRS])
        eps = sb("eps", [P, BATCH * ROWPAIRS])
        counts = sb("counts", [P, 4])
        TILE = 4 * CHANNELS
        xm = xs[:, 0, :].rearrange("p (r j c) -> p r j c", r=2, j=4)
        xh = xs[:, 1, :].rearrange("p (r j c) -> p r j c", r=2, j=4)
        g = xn[:, :, :].rearrange("p a (k t) -> p (a k) t", t=TOKENS)
        om = res[:, 0, :].rearrange("p (r j c) -> p r j c", r=2, j=4)
        mt = res[:, 1, :].rearrange("p (r k t) -> p r k t", r=2, k=KC)

        ps = ctx.enter_context(nc.psum_tensor("ps", [P, 8, 512], F32))
        T_BANK, F2_BANK, M1_BANK, M2_BANK, F5_BANK = range(5)
        F1_BANKS, TT_BANKS, F6_BANKS = (5, 6), (7, 0), (1, 2)
        MM1_BANKS, MM2_BANKS = (3, 4), (5, 6)

        s_const, s_wts, s_pad = sem("s_const"), sem("s_wts"), sem("s_pad")
        x_loaded = [sem("x_loaded0"), sem("x_loaded1")]
        stored = [sem("stored0"), sem("stored1")]
        w_loaded, w_ready = sem("w_loaded"), sem("w_ready")
        f1_done, t_done, f2_done, m1_done = sem("f1_done"), sem("t_done"), sem("f2_done"), sem("m1_done")
        m2_done, f5_done, tt_done, f6_done = sem("m2_done"), sem("f5_done"), sem("tt_done"), sem("f6_done")
        y_ready, z_ready, zf_ready, h_ready = sem("y_ready"), sem("z_ready"), sem("zf_ready"), sem("h_ready")
        clamped, u_ready, v_ready = sem("clamped"), sem("u_ready"), sem("v_ready")
        vt_ready, res_ready = sem("vt_ready"), sem("res_ready")
        ln_step, xn_ready, sum_ready = sem("ln_step"), sem("xn_ready"), sem("sum_ready")
        a_loaded = [sem("a_loaded0"), sem("a_loaded1")]
        st_done, mv_step, mv_ready, rs_step, rstd_ready = sem("st_done"), sem("mv_step"), sem("mv_ready"), sem("rs_step"), sem("rstd_ready")
        m_loaded = [sem("m_loaded0"), sem("m_loaded1")]
        m_stored = [sem("m_stored0"), sem("m_stored1")]
        st2_done, mv2_ready, rs2_step, rstd2_ready = sem("st2_done"), sem("mv2_ready"), sem("rs2_step"), sem("rstd2_ready")
        xh_ready, skip_ready = sem("xh_ready"), sem("skip_ready")
        mt_done, mt_ready, mm1_done, g_ready = sem("mt_done"), sem("mt_ready"), sem("mm1_done"), sem("g_ready")
        mm2_done, om_ready = sem("mm2_done"), sem("om_ready")

        def basis(col, width=P):
            return const[:, col:col + width]

        ident = basis(C_ID)

        def unit_view(a, b, i):
            return a[b].rearrange("(r p) c -> p r c", p=P)[:, :, bass.ds(i * PAIR, PAIR)]

        def tile_view(a, n):
            return a.rearrange("b (n j p) c -> p (b n) j c", p=P, j=4)[:, bass.ds(n, 1)].rearrange("p o j c -> p (o j) c")

        block = ctx.enter_context(nc.Block())

        @block.sync
        def _(sp):
            sp.dma_start(const[:, :], consts).then_inc(s_const, 16)

            def load_weights(L, i):
                sp.dma_start(wstage[:, :, :],
                             spectral[L.index].rearrange("(g k) p n -> p g k n", k=2)[:, bass.ds(i, 1)]
                             .rearrange("p o k n -> p (o k) n")).then_inc(w_loaded, 16)

            def load_unit(L, b, i):
                sp.dma_start(xs[:, b, :].rearrange("p (r c) -> p r c", c=PAIR),
                             unit_view(layer_in[L.index], b, i)).then_inc(x_loaded[b], 16)

            def spectral_layer(L):
                load_weights(L, 0)
                for b in range(BATCH):
                    load_unit(L, b, 0)

                def body(i, last):
                    if not last:
                        sp.wait_ge(w_ready, 5 * (PAIRS * L.index + 1) + i * 5)
                        load_weights(L, i + 1)
                    for b in range(BATCH):
                        sp.wait_ge(res_ready, CHUNKS * (L.units + b + 1) + i * (2 * CHUNKS))
                        sp.dma_start(unit_view(layer_out[L.index], b, i),
                                     res[:, b, :].rearrange("p (r c) -> p r c", c=PAIR)).then_inc(stored[b], 16)
                        if not last:
                            load_unit(L, b, i + 1)

                iterate(sp, PAIRS, body, L.index == 0)
                for b in range(BATCH):
                    sp.wait_ge(stored[b], 16 * PAIRS * (L.index + 1))

            def statistics_loads():
                for r in range(2):
                    sp.dma_start(xm[:, r], tile_view(after[0], r)).then_inc(a_loaded[r], 16)
                with sp.Fori(0, TILES // 2 - 1) as i:
                    for r in range(2):
                        sp.wait_ge(st_done, 4 * (r + 1) + i * 8)
                        sp.dma_start(xm[:, r], tile_view(after[0], 2 * i + (2 + r))).then_inc(a_loaded[r], 16)
                sp.wait_ge(st_done, 4 * TILES)

            def token_mlp_moves():
                for r in range(2):
                    sp.dma_start(xm[:, r], tile_view(after[1], r)).then_inc(m_loaded[r], 16)

                def body(i, last):
                    for r in range(2):
                        sp.wait_ge(om_ready, 4 * (r + 1) + i * 8)
                        sp.dma_start(tile_view(after[2], 2 * i + r), om[:, r]).then_inc(m_stored[r], 16)
                        if not last:
                            sp.dma_start(xm[:, r], tile_view(after[1], 2 * i + (2 + r))).then_inc(m_loaded[r], 16)

                iterate(sp, TILES // 2, body, True)
                for r in range(2):
                    sp.wait_ge(m_stored[r], 16 * TILES // 2)

            spectral_layer(layers[0])
            statistics_loads()
            sp.dma_start(lnrow[:, :, :], ln1.rearrange("a c -> (a c)").partition_broadcast(P)
                         .rearrange("p (a c) -> p a c", a=2)).then_inc(s_wts, 16)
            sp.dma_start(b2row[:, :], b2.partition_broadcast(P)).then_inc(s_wts, 16)
            sp.dma_start(colp[:, :], cols).then_inc(s_wts, 16)
            sp.dma_start(w1s[:, :, :], w1.rearrange("(k p) n -> p k n", p=P)).then_inc(s_wts, 16)
            sp.dma_start(w2s[:, :, :], w2.rearrange("(k p) n -> p k n", p=P)).then_inc(s_wts, 16)
            spectral_layer(layers[1])
            token_mlp_moves()
            spectral_layer(layers[2])
            spectral_layer(layers[3])

        @block.tensor
        def _(pe):
            pe.wait_ge(s_const, 16)
            pe.wait_ge(s_pad, 1)

            def f1(L, b, i):
                if L.norm:
                    pe.wait_ge(xn_ready, b + 1 + i * 2)
                else:
                    pe.wait_ge(x_loaded[b], 16 * (PAIRS * L.index + 1) + i * 16)
                src = xn if L.norm else xs
                for k in range(CHUNKS):
                    if k >= 2:
                        pe.wait_ge(y_ready, CHUNKS * (L.units + b) + k - 1 + i * (2 * CHUNKS))
                    for j in range(CHUNK):
                        r = CHUNK * k + j
                        mm = pe.matmul(ps[0:PAIR, F1_BANKS[k % 2], j * P:(j + 1) * P],
                                       src[:, b, r * PAIR:(r + 1) * PAIR], basis(C_D1), start=True, stop=True)
                    mm.then_inc(f1_done, 1)

            def chain(L, b, i):
                done = L.chain + b * L.n
                step = 2 * L.n
                for t in range(L.n + 4):
                    k = t - 4
                    if 0 <= k < L.n:
                        pe.wait_ge(u_ready, done + k + 1 + i * step)
                        if k >= 1:
                            pe.wait_ge(v_ready, done + k + i * step)
                        for item, col, width, to, first, final in L.groups[k][4]:
                            mm = pe.matmul(ps[0:PAIR, F5_BANK, to:to + width], u[:, k % 2, item, :],
                                           basis(col, width), start=first, stop=final)
                        mm.then_inc(f5_done, 1)
                    k = t - 3
                    if 0 <= k < L.n:
                        pe.wait_ge(h_ready, 2 * (done + k + 1) + i * (2 * step))
                        for item in range(L.groups[k][3]):
                            for n in range(2):
                                for ri in range(2):
                                    to = item * PAIR + n * BLOCK
                                    mm = pe.matmul(ps[ri * SIDE:(ri + 1) * SIDE, M2_BANK, to:to + BLOCK],
                                                   h[:, k % 2, n, item * SIDE:(item + 1) * SIDE],
                                                   w[:, n, P + ri * BLOCK:P + (ri + 1) * BLOCK],
                                                   start=True, stop=True)
                        mm.then_inc(m2_done, 1)
                    k = t - 2
                    if 0 <= k < L.n:
                        pe.wait_ge(zf_ready, done + k + 1 + i * step)
                        if k == 0 and b == 0:
                            pe.wait_ge(w_ready, 5 * (PAIRS * L.index + 1) + i * 5)
                        width = len(L.groups[k][2]) * L.kh
                        for n in range(2):
                            mm = pe.matmul(ps[:, M1_BANK, n * 256:n * 256 + width], w[:, n, 0:P],
                                           zf[:, k % 2, n, 0:width], start=True, stop=True)
                        mm.then_inc(m1_done, 1)
                    k = t - 1
                    if 0 <= k < L.n:
                        pe.wait_ge(z_ready, done + k + 1 + i * step)
                        if k == 0:
                            wait_past(pe, res_ready, CHUNKS * (L.units + b) + i * (2 * CHUNKS))
                        for m, (slot, col) in enumerate(L.groups[k][2]):
                            for n in range(2):
                                for ri in range(2):
                                    to = n * 256 + m * L.kh
                                    at = slot * PAIR + n * BLOCK
                                    mm = pe.matmul(ps[ri * SIDE:(ri + 1) * SIDE, F2_BANK, to:to + L.kh],
                                                   z[:, k % 2, at:at + SIDE],
                                                   basis(col + ri * SIDE, L.kh), start=True, stop=True)
                        mm.then_inc(f2_done, 1)
                    k = t
                    if k < L.n:
                        if k == 0:
                            pe.wait_ge(y_ready, CHUNKS * (L.units + b + 1) + i * (2 * CHUNKS))
                        s0, slots = L.groups[k][0:2]
                        for j in range(slots):
                            mm = pe.transpose(ps[:, T_BANK, j * PAIR:(j + 1) * PAIR],
                                              y[0:PAIR, s0 + j].rearrange("p a b -> p (a b)"),
                                              ident[0:PAIR, 0:PAIR])
                        mm.then_inc(t_done, 1)

            def post(L, b, i):
                pe.wait_ge(v_ready, L.chain + (b + 1) * L.n + i * (2 * L.n))
                base = CHUNKS * (L.units + b)
                for t in range(CHUNKS + 1):
                    k = t
                    if k < CHUNKS:
                        if k >= 2:
                            pe.wait_ge(vt_ready, base + k - 1 + i * (2 * CHUNKS))
                        for j in range(CHUNK):
                            r = 2 * (CHUNK * k + j)
                            mm = pe.transpose(ps[:, TT_BANKS[k % 2], j * PAIR:(j + 1) * PAIR],
                                              v[0:PAIR, r:r + 2].rearrange("p a b c -> p (a b c)"),
                                              ident[0:PAIR, 0:PAIR])
                        mm.then_inc(tt_done, 1)
                    k = t - 1
                    if k >= 0:
                        pe.wait_ge(vt_ready, base + k + 1 + i * (2 * CHUNKS))
                        if k >= 2:
                            pe.wait_ge(res_ready, base + k - 1 + i * (2 * CHUNKS))
                        pe.matmul(ps[:, F6_BANKS[k % 2], 0:CHUNK * PAIR], basis(C_D6), vt[:, k % 2, :],
                                  start=True, stop=True).then_inc(f6_done, 1)

            def spectral_layer(L):
                f1(L, 0, 0)

                def body(i, last):
                    chain(L, 0, i)
                    f1(L, 1, i)
                    post(L, 0, i)
                    chain(L, 1, i)
                    if not last:
                        f1(L, 0, i + 1)
                    post(L, 1, i)

                iterate(pe, PAIRS, body, L.index == 0)

            def token_mlp():
                def turn(r, i):
                    pe.wait_ge(xh_ready, 4 * (r + 1) + i * 8)
                    for k in range(KC):
                        for j in range(4):
                            mm = pe.transpose(ps[:, k, j * P:(j + 1) * P], xh[:, r, j, k * P:(k + 1) * P], ident)
                        mm.then_inc(mt_done, 1)

                def first(r, i):
                    pe.wait_ge(mt_ready, KC * (r + 1) + i * (2 * KC))
                    for n in range(HC):
                        if n >= 2:
                            pe.wait_ge(g_ready, HC * r + n - 1 + i * (2 * HC))
                        for k in range(KC):
                            mm = pe.matmul(ps[:, MM1_BANKS[n % 2], :], w1s[:, k, n * P:(n + 1) * P], mt[:, r, k, :],
                                           start=k == 0, stop=k == KC - 1)
                        mm.then_inc(mm1_done, 1)

                def second(r, i):
                    pe.wait_ge(g_ready, HC * (r + 1) + i * (2 * HC))
                    for j in range(4):
                        if j >= 2:
                            pe.wait_ge(om_ready, 4 * r + j - 1 + i * 8)
                        elif j == 0:
                            wait_past(pe, om_ready, 4 * r + i * 8)
                        for n in range(HC):
                            mm = pe.matmul(ps[:, MM2_BANKS[j % 2], 0:CHANNELS], g[:, n, j * P:(j + 1) * P], w2s[:, n, :],
                                           start=n == 0, stop=n == HC - 1)
                        mm.then_inc(mm2_done, 1)

                def body(i, last):
                    first(0, i)
                    turn(1, i)
                    second(0, i)
                    first(1, i)
                    if not last:
                        turn(0, i + 1)
                    second(1, i)

                turn(0, 0)
                iterate(pe, TILES // 2, body, True)

            spectral_layer(layers[0])
            spectral_layer(layers[1])
            pe.wait_ge(s_wts, 80)
            token_mlp()
            spectral_layer(layers[2])
            spectral_layer(layers[3])

        @block.scalar
        def _(act):
            def f1(L, b, i):
                for k in range(CHUNKS):
                    act.wait_ge(f1_done, CHUNKS * (L.units + b) + k + 1 + i * (2 * CHUNKS))
                    r = 2 * CHUNK * k
                    act.activation(y[0:PAIR].rearrange("p k a r -> p r a k")[:, r:r + 2 * CHUNK],
                                   ps[0:PAIR, F1_BANKS[k % 2], :].rearrange("p (r a k) -> p r a k", a=2, k=HALF),
                                   ACT.Copy).then_inc(y_ready, 1)

            def chain(L, b, i):
                done = L.chain + b * L.n
                step = 2 * L.n
                for t in range(L.n + 4):
                    k = t - 4
                    if 0 <= k < L.n:
                        act.wait_ge(f5_done, done + k + 1 + i * step)
                        s0, slots = L.groups[k][0:2]
                        act.activation(v[0:PAIR].rearrange("p r a k -> p k a r")[:, s0:s0 + slots],
                                       ps[0:PAIR, F5_BANK, 0:slots * P].rearrange("p (k a r) -> p k a r", a=2, r=SIDE),
                                       ACT.Copy, scale=L.inverse).then_inc(v_ready, 1)
                    k = t - 2
                    if 0 <= k < L.n:
                        act.wait_ge(m1_done, done + k + 1 + i * step)
                        width = len(L.groups[k][2]) * L.kh
                        for n in range(2):
                            act.activation(h[:, k % 2, n, 0:width], ps[:, M1_BANK, n * 256:n * 256 + width],
                                           L.act, bias=w[:, n, W_COLS - 1:W_COLS]).then_inc(h_ready, 1)
                    k = t
                    if k < L.n:
                        act.wait_ge(t_done, done + k + 1 + i * step)
                        n = L.groups[k][1] * PAIR
                        act.activation(z[:, k % 2, 0:n], ps[:, T_BANK, 0:n], ACT.Copy).then_inc(z_ready, 1)

            def spectral_layer(L):
                f1(L, 0, 0)

                def body(i, last):
                    chain(L, 0, i)
                    f1(L, 1, i)
                    chain(L, 1, i)
                    if not last:
                        f1(L, 0, i + 1)

                iterate(act, PAIRS, body, L.index == 0)

            def token_mlp():
                def turn(r, i):
                    for k in range(KC):
                        act.wait_ge(mt_done, KC * r + k + 1 + i * (2 * KC))
                        act.activation(mt[:, r, k, :], ps[:, k, :], ACT.Identity, scale=colp[:, HC + k:HC + k + 1],
                                       bias=colp[:, HC + KC + k:HC + KC + k + 1]).then_inc(mt_ready, 1)

                def first(r, i):
                    for n in range(HC):
                        act.wait_ge(mm1_done, HC * r + n + 1 + i * (2 * HC))
                        act.activation(g[:, n, :], ps[:, MM1_BANKS[n % 2], :], ACT.Gelu,
                                       bias=colp[:, n:n + 1]).then_inc(g_ready, 1)

                def body(i, last):
                    first(0, i)
                    turn(1, i)
                    first(1, i)
                    if not last:
                        turn(0, i + 1)

                turn(0, 0)
                iterate(act, TILES // 2, body, True)

            spectral_layer(layers[0])
            spectral_layer(layers[1])
            act.wait_ge(s_wts, 80)
            token_mlp()
            spectral_layer(layers[2])
            spectral_layer(layers[3])

        @block.vector
        def _(dve):
            dve.memset(z[:, :, :], 0.0).then_inc(s_pad, 1)

            def chain(L, b, i):
                done = L.chain + b * L.n
                step = 2 * L.n
                shrunk = done if L.index == 0 else done - 2 * PAIRS * layers[1].n
                for t in range(L.n + 4):
                    k = t - 3
                    if 0 <= k < L.n:
                        dve.wait_ge(m2_done, done + k + 1 + i * step)
                        n = L.groups[k][3] * PAIR
                        to = u[:, k % 2].rearrange("p a c -> p (a c)")[:, 0:n]
                        if L.shrink:
                            dve.tensor_scalar(clamp[:, k % 2, 0:n], ps[:, M2_BANK, 0:n], LAMBDA, -LAMBDA,
                                              ALU.min, ALU.max).then_inc(clamped, 1)
                            dve.wait_ge(clamped, shrunk + k + 1 + i * step)
                            dve.tensor_tensor(to, ps[:, M2_BANK, 0:n], clamp[:, k % 2, 0:n],
                                              ALU.subtract).then_inc(u_ready, 1)
                        else:
                            dve.tensor_copy(to, ps[:, M2_BANK, 0:n]).then_inc(u_ready, 1)
                    k = t - 1
                    if 0 <= k < L.n:
                        dve.wait_ge(f2_done, done + k + 1 + i * step)
                        n = len(L.groups[k][2]) * L.kh
                        dve.tensor_scalar(zf[:, k % 2, :, 0:n],
                                          ps[:, F2_BANK, :].rearrange("p (n m) -> p n m", n=2)[:, :, 0:n],
                                          L.forward, None, ALU.mult).then_inc(zf_ready, 1)

            def post(L, b, i):
                base = CHUNKS * (L.units + b)
                if L.norm:
                    dve.wait_ge(sum_ready, b + 1 + i * 2)
                else:
                    dve.wait_ge(x_loaded[b], 16 * (PAIRS * L.index + 1) + i * 16)
                wait_past(dve, stored[b], 16 * PAIRS * L.index + i * 16)
                for t in range(CHUNKS + 1):
                    k = t
                    if k < CHUNKS:
                        dve.wait_ge(tt_done, base + k + 1 + i * (2 * CHUNKS))
                        dve.tensor_copy(vt[:, k % 2, :], ps[:, TT_BANKS[k % 2], 0:CHUNK * PAIR]).then_inc(vt_ready, 1)
                    k = t - 1
                    if k >= 0:
                        dve.wait_ge(f6_done, base + k + 1 + i * (2 * CHUNKS))
                        at = slice(k * CHUNK * PAIR, (k + 1) * CHUNK * PAIR)
                        dve.tensor_tensor(res[:, b, at], ps[:, F6_BANKS[k % 2], 0:CHUNK * PAIR], xs[:, b, at],
                                          ALU.add).then_inc(res_ready, 1)

            def spectral_layer(L):
                def body(i, last):
                    chain(L, 0, i)
                    post(L, 0, i)
                    chain(L, 1, i)
                    post(L, 1, i)

                iterate(dve, PAIRS, body, L.index == 0)

            def statistics():
                with dve.Fori(0, TILES // 2) as i:
                    for r in range(2):
                        dve.wait_ge(a_loaded[r], 16 + i * 16)
                        for j in range(4):
                            dve.bn_stats(stat[:, r, j, :], xm[:, r, j, :]).then_inc(st_done, 1)
                        dve.wait_ge(st_done, 4 * (r + 1) + i * 8)
                        dve.tensor_copy(counts[:, :], stat[:, r, :, 0])
                        for j in range(4):
                            dve.bn_aggr(mv2[:, r, j, :], stat[:, r, j, :]).then_inc(mv_step, 1)
                        dve.wait_ge(mv_step, 4 * (r + 1) + i * 8)
                        dve.tensor_copy(mv[:, bass.ds(i * 8 + 4 * r, 4), :], mv2[:, r]).then_inc(mv_ready, 1)

            def token_mlp():
                def normalise(r, i):
                    dve.wait_ge(m_loaded[r], 16 + i * 16)
                    for j in range(4):
                        dve.bn_stats(stat[:, r, j, :], xm[:, r, j, :]).then_inc(st2_done, 1)
                    dve.wait_ge(st2_done, 4 * (r + 1) + i * 8)
                    dve.tensor_copy(counts[:, :], stat[:, r, :, 0])
                    for j in range(4):
                        dve.bn_aggr(mv2[:, r, j, :], stat[:, r, j, :]).then_inc(mv2_ready, 1)
                    dve.wait_ge(mv2_ready, 4 * (r + 1) + i * 8)
                    dve.wait_ge(rstd2_ready, r + 1 + i * 2)
                    for j in range(4):
                        dve.tensor_scalar(xh[:, r, j, :], xm[:, r, j, :], mv2[:, r, j, 0:1], rstd2[:, r, j:j + 1],
                                          ALU.subtract, ALU.mult).then_inc(xh_ready, 1)

                def results(r, i):
                    dve.wait_ge(skip_ready, r + 1 + i * 2)
                    wait_past(dve, m_stored[r], i * 16)
                    for j in range(4):
                        dve.wait_ge(mm2_done, 4 * r + j + 1 + i * 8)
                        dve.tensor_tensor(om[:, r, j, :], ps[:, MM2_BANKS[j % 2], 0:CHANNELS], xm[:, r, j, :],
                                          ALU.add).then_inc(om_ready, 1)

                def body(i, last):
                    normalise(1, i)
                    results(0, i)
                    if not last:
                        normalise(0, i + 1)
                    results(1, i)

                normalise(0, 0)
                iterate(dve, TILES // 2, body, True)

            spectral_layer(layers[0])
            statistics()
            spectral_layer(layers[1])
            token_mlp()
            spectral_layer(layers[2])
            spectral_layer(layers[3])

        @block.gpsimd
        def _(pool):
            pool.memset(power[:, :], -0.5).then_inc(rs_step, 1)
            pool.memset(eps[:, :], LN_EPS).then_inc(rs_step, 1)
            pool.wait_ge(s_const, 16)

            def weights(L, i):
                pool.wait_ge(w_loaded, 16 * (PAIRS * L.index + 1) + i * 16)
                wait_past(pool, m2_done, L.chain + i * (2 * L.n))
                real = C_SIGN + (1 if L.act == ACT.Gelu else 0)
                pool.tensor_tensor(w[:, :, 0:SIDE], wstage[:, :, 0:SIDE],
                                   const[:, C_SIGN:C_SIGN + 1].unsqueeze(1).to_broadcast([P, 2, SIDE]),
                                   ALU.mult).then_inc(w_ready, 1)
                pool.tensor_copy(w[:, :, SIDE:P], wstage[:, :, SIDE:P]).then_inc(w_ready, 1)
                pool.tensor_scalar(w[:, :, P:P + BLOCK], wstage[:, :, P:P + BLOCK], const[:, real:real + 1], None,
                                   ALU.mult).then_inc(w_ready, 1)
                imag = wstage[:, :, P + BLOCK:P + PAIR]
                if L.act == ACT.Gelu:
                    pool.tensor_scalar(w[:, :, P + BLOCK:P + PAIR], imag, const[:, C_SIGN + 2:C_SIGN + 3], None,
                                       ALU.mult).then_inc(w_ready, 1)
                else:
                    pool.tensor_copy(w[:, :, P + BLOCK:P + PAIR], imag).then_inc(w_ready, 1)
                pool.tensor_copy(w[:, :, W_COLS - 1:], wstage[:, :, W_COLS - 1:]).then_inc(w_ready, 1)

            def layer_norm(b, i):
                pool.wait_ge(x_loaded[b], 16 * (PAIRS + 1) + i * 16)
                xv = xs[:, b, :].rearrange("p (r c) -> p r c", c=PAIR)
                xo = xn[:, b, :].rearrange("p (r c) -> p r c", c=PAIR)
                rows = slice(b * ROWPAIRS, (b + 1) * ROWPAIRS)
                mean = mv[:, rows, 0:1].to_broadcast([P, ROWPAIRS, PAIR])
                scale = rstd[:, rows].unsqueeze(2).to_broadcast([P, ROWPAIRS, PAIR])
                gain = lnrow[:, 0:1, bass.ds(i * PAIR, PAIR)].to_broadcast([P, ROWPAIRS, PAIR])
                shift = lnrow[:, 1:2, bass.ds(i * PAIR, PAIR)].to_broadcast([P, ROWPAIRS, PAIR])
                at = 3 * b
                pool.tensor_tensor(xo, xv, mean, ALU.subtract).then_inc(ln_step, 1)
                pool.wait_ge(ln_step, at + 1 + i * 6)
                pool.tensor_tensor(xo, xo, scale, ALU.mult).then_inc(ln_step, 1)
                pool.wait_ge(ln_step, at + 2 + i * 6)
                pool.tensor_tensor(xo, xo, gain, ALU.mult).then_inc(ln_step, 1)
                pool.wait_ge(ln_step, at + 3 + i * 6)
                pool.tensor_tensor(xo, xo, shift, ALU.add).then_inc(xn_ready, 1)
                pool.wait_ge(xn_ready, b + 1 + i * 2)
                pool.tensor_tensor(xv, xv, xo, ALU.add).then_inc(sum_ready, 1)

            def spectral_layer(L):
                if L.norm:
                    layer_norm(0, 0)

                def body(i, last):
                    weights(L, i)
                    if L.norm:
                        layer_norm(1, i)
                        if not last:
                            layer_norm(0, i + 1)

                iterate(pool, PAIRS, body, L.index == 0)

            def root():
                pool.wait_ge(mv_ready, TILES)
                pool.tensor_tensor(rstd[:, :], mv[:, :, 1], eps[:, :], ALU.add).then_inc(rs_step, 1)
                pool.wait_ge(rs_step, 3)
                pool.tensor_tensor(rstd[:, :], rstd[:, :], power[:, :], ALU.pow).then_inc(rstd_ready, 1)
                pool.wait_ge(rstd_ready, 1)

            def token_mlp():
                def root2(r, i):
                    pool.wait_ge(mv2_ready, 4 * (r + 1) + i * 8)
                    pool.tensor_tensor(rstd2[:, r, :], mv2[:, r, :, 1], eps[:, 0:4], ALU.add).then_inc(rs2_step, 1)
                    pool.wait_ge(rs2_step, r + 1 + i * 2)
                    pool.tensor_tensor(rstd2[:, r, :], rstd2[:, r, :], power[:, 0:4], ALU.pow).then_inc(rstd2_ready, 1)
                    pool.wait_ge(xh_ready, 4 * (r + 1) + i * 8)
                    pool.tensor_tensor(xm[:, r], xm[:, r], b2row[:, :].unsqueeze(1).to_broadcast([P, 4, CHANNELS]),
                                       ALU.add).then_inc(skip_ready, 1)

                with pool.Fori(0, TILES // 2) as i:
                    root2(0, i)
                    root2(1, i)

            spectral_layer(layers[0])
            root()
            pool.wait_ge(s_wts, 80)
            spectral_layer(layers[1])
            token_mlp()
            spectral_layer(layers[2])
            spectral_layer(layers[3])


def host_constants():
    import numpy as np
    n, f = np.arange(SIDE), 2 * np.pi / SIDE
    half = np.arange(HALF)
    col = np.stack([np.cos(f * np.outer(n, half)), -np.sin(f * np.outer(n, half))], 1)
    col[:, 1, 0] = (-1.0) ** n
    d1 = np.kron(np.eye(2), col.reshape(SIDE, SIDE))
    inv = 2 * col.transpose(1, 2, 0)
    inv[:, 0] /= 2
    d6 = np.kron(np.eye(2), inv.reshape(SIDE, SIDE))
    c, s = np.cos(f * np.outer(n, n)), np.sin(f * np.outer(n, n))
    o = np.zeros((SIDE, SIDE))
    d2 = np.block([[c, -s], [s, c]])
    d2a, d2b = np.block([[c, -s], [o, o]]), np.block([[o, o], [c, -s]])
    d5 = np.block([[c, s], [-s, c]])
    d5a, d5b = np.block([[c, o], [-s, o]]), np.block([[o, c], [o, -s]])

    def pair(first):
        m = np.zeros((2, 2, HALF, 2, 2 * SIDE))
        for slot, d in enumerate((first, d5)):
            m[:, slot, :, slot, :] = d.reshape(2, SIDE, 2 * SIDE)[:, :HALF]
        return m.reshape(P, 4 * SIDE)

    sign = np.ones((P, 3))
    sign[SIDE:, 0:2] = -1
    sign[ONE_ROW, 1:] = 1 / ONE_GELU
    return np.concatenate([d1, np.eye(P), d2, d2a, d2b, d5, d5a, d5b, d6, pair(d5), pair(d5a), sign],
                          1).astype(np.float32)


def pack_spectral(w1, b1, w2, b2, one):
    import numpy as np
    t = np.zeros((BLOCKS, 2, SIDE, W_COLS), np.float32)
    for row in range(2):
        for to in range(2):
            t[:, row, :BLOCK, to * SIDE:to * SIDE + BLOCK] = w1[row ^ to]
            t[:, row, :BLOCK, P + to * BLOCK:P + (to + 1) * BLOCK] = w2[row ^ to]
        t[:, 0, ONE_ROW, P + row * BLOCK:P + (row + 1) * BLOCK] = b2[row]
        t[:, row, :BLOCK, W_COLS - 1] = b1[row]
    t[:, 0, ONE_ROW, W_COLS - 1] = one
    return t.reshape(BLOCKS, P, W_COLS)


def kernel(**inputs):
    import numpy as np
    import concourse.bacc as bacc
    from concourse.bass_utils import run_bass_kernel_spmd

    a = {k: np.asarray(t) for k, t in inputs.items()}

    def all_blocks(t):
        return np.broadcast_to(t, (BLOCKS,) + t.shape)

    spectral = np.stack([
        pack_spectral(a["L0_conv_w1"], a["L0_conv_b1"], a["L0_conv_w2"], a["L0_conv_b2"], 1.0),
        pack_spectral(a["L1_conv_w1"], a["L1_conv_b1"], a["L1_conv_w2"], a["L1_conv_b2"], ONE_GELU),
        pack_spectral([all_blocks(a["L2_conv_w1r"].T), all_blocks(a["L2_conv_w1i"].T)],
                      [all_blocks(a["L2_conv_b1"][:, n]) for n in range(2)],
                      [all_blocks(a["L2_conv_w2r"].T), all_blocks(a["L2_conv_w2i"].T)],
                      [all_blocks(a["L2_conv_b2"][:, n]) for n in range(2)], 1.0),
        pack_spectral([a["L3_conv_w1"][..., n] for n in range(2)], [a["L3_conv_b1"][..., n] for n in range(2)],
                      [a["L3_conv_w2"][..., n] for n in range(2)], [a["L3_conv_b2"][..., n] for n in range(2)], 1.0)])
    arrays = {
        "x": a["x"].reshape(BATCH, SIDE * SIDE, CHANNELS),
        "consts": host_constants(),
        "spectral": spectral,
        "ln1": np.stack([a["L1_conv_ln1_g"], a["L1_conv_ln1_b"]]),
        "cols": np.concatenate([a["L1_conv_mlp_b1"].reshape(HC, P), a["L1_conv_ln2_g"].reshape(KC, P),
                                a["L1_conv_ln2_b"].reshape(KC, P)]).T,
        "w1": a["L1_conv_mlp_w1"],
        "w2": a["L1_conv_mlp_w2"],
        "b2": a["L1_conv_mlp_b2"],
    }
    arrays = {f"in_{k}": np.ascontiguousarray(t) for k, t in arrays.items()}
    nc = bacc.Bacc("TRN2", target_bir_lowering=False, num_devices=1)
    args = [nc.dram_tensor(k, t.shape, mybir.dt.from_np(t.dtype), kind="ExternalInput").ap() for k, t in arrays.items()]
    out = nc.dram_tensor("out", (BATCH, SIDE * SIDE, CHANNELS), F32, kind="ExternalOutput").ap()
    build(nc, *args, out)
    r = run_bass_kernel_spmd(nc, [arrays], core_ids=[0])
    return np.asarray(r.results[0]["out"]).reshape(BATCH, SIDE, SIDE, CHANNELS)
```

```python
from contextlib import ExitStack

import concourse.bass as bass
from concourse import mybir

ALU = mybir.AluOpType
ACT = mybir.ActivationFunctionType
F32 = mybir.dt.float32
F32R = mybir.dt.float32r

P = 128
BATCH, SIDE, CHANNELS = 2, 64, 384
BLOCKS, BLOCK = 8, 48
PAIR = 2 * BLOCK
PAIRS = CHANNELS // PAIR
ROWPAIRS = SIDE * SIDE // P
CHUNK = 4
CHUNKS = ROWPAIRS // CHUNK
HALF = SIDE // 2
HIDDEN = 4 * CHANNELS
KC, HC = CHANNELS // P, HIDDEN // P
TOKENS = 4 * P
TILES = BATCH * SIDE * SIDE // TOKENS
LAG = 2
WPART = 2 * CHANNELS
WPARTS = KC * HIDDEN // WPART
LAMBDA = 0.01
ONE_ROW = PAIR
ONE_GELU = 8.0
LN_EPS = 1e-5

(C_D1, C_ID, C_D2, C_D2A, C_D2B, C_D5, C_D5A, C_D5B, C_D6) = [P * n for n in range(9)]
C_D5P, C_D5P0, C_SIGN = 9 * P, 11 * P, 13 * P
C_COLS = 13 * P + 5
ROWS = PAIR + 1
SECOND, BIAS = ROWS, ROWS + PAIR
W_COLS = BIAS + 1
HALVES = 2
HALF_CHUNKS = CHUNKS // HALVES
STAGES = 6
POST_BESIDE = ((1, 2, 3), (4, 5, 6), (7, 8))
F1_BESIDE = ((0,), (1,), (2, 3), (4, 5), (6, 7))


class Layer:

    def __init__(self, index, kh, forward, inverse, act, shrink, norm, chain_base):
        self.index, self.kh = index, kh
        self.forward, self.inverse = forward, inverse
        self.act, self.shrink, self.norm = act, shrink, norm
        if kh == SIDE:
            self.groups = [(0, 1, 1, [(0, SIDE, C_D2A, [0]), (SIDE, SIDE, C_D2B, [0])],
                            [(0, 0, C_D5A, P, 0, True, False), (1, 0, C_D5B, P, 0, False, True)])]
            for s in range(1, HALF, 4):
                n = min(4, HALF - s)
                self.groups.append((s, n, 2, [(0, SIDE, C_D2, [0, 2]), (SIDE, SIDE, C_D2, [1, min(3, n - 1)])],
                                    [(j % 2, j // 2, C_D5, P, j * P, True, True) for j in range(n)]))
        else:
            self.groups = []
            for s in range(0, HALF, 4):
                rows = [(j * HALF, HALF, C_D2A if s + j == 0 else C_D2, [j]) for j in range(4)]
                items = [(j, 0, C_D5P0 if s + j == 0 else C_D5P, 2 * P, 2 * j * P, True, True) for j in range(2)]
                self.groups.append((s, 4, 1, rows, items))
        self.units = index * 2 * PAIRS
        self.chain = chain_base
        self.n = len(self.groups)


def iterate(engine, count, body):
    body(0, False)
    with engine.Fori(1, count - 1) as i:
        body(i, False)
    body(count - 1, True)


def first_of(i):
    return isinstance(i, int) and i == 0


def wait_past(engine, semaphore, value):
    if not isinstance(value, int) or value > 0:
        engine.wait_ge(semaphore, value)


def make_layers():
    layers, base = [], 0
    for index, (kh, fwd, inv, act, shrink, norm) in enumerate([
            (SIDE, 1.0, 1.0 / (SIDE * SIDE), ACT.Relu, True, False),
            (HALF, 1.0 / SIDE, 1.0 / SIDE, ACT.Gelu, False, True),
            (SIDE, 1.0 / SIDE, 1.0 / SIDE, ACT.Relu, True, False),
            (SIDE, 1.0 / SIDE, 1.0 / SIDE, ACT.Relu, True, False)]):
        layers.append(Layer(index, kh, fwd, inv, act, shrink, norm, base))
        base += 2 * PAIRS * layers[-1].n
    return layers


def build(nc, x, consts, spectral, ln1, lncol_in, cols, w1, w2, b2, out):
    layers = make_layers()
    with ExitStack() as ctx:
        def sb(name, shape):
            return ctx.enter_context(nc.sbuf_tensor(name, shape, F32))

        def sbr(name, shape):
            return ctx.enter_context(nc.sbuf_tensor(name, shape, F32R))

        def sem(name):
            return ctx.enter_context(nc.semaphore(name))

        after = [nc.dram_tensor(f"after_{n}", (BATCH, SIDE * SIDE, CHANNELS), F32).ap() for n in range(4)]
        layer_in = [x, after[0], after[2], after[3]]
        layer_out = [after[0], after[1], after[3], out]

        UNIT = ROWPAIRS * PAIR
        const = sb("const", [P, C_COLS])
        lnrow = sb("lnrow", [P, 2, CHANNELS])
        lncol = sb("lncol", [P, PAIRS, 2])
        gcol = sb("gcol", [P, 2])
        b2row = sb("b2row", [P, CHANNELS])
        colp = sb("colp", [P, HC + 2 * KC])
        stat = sb("stat", [P, 2, 4, 6])
        mv = sb("mv", [P, BATCH * ROWPAIRS, 2])
        rstd = sb("rstd", [P, BATCH * ROWPAIRS])
        mv2 = sb("mv2", [P, 2, 4, 2])
        rstd2 = sb("rstd2", [P, 2, 4])
        power = sb("power", [P, BATCH * ROWPAIRS])
        eps = sb("eps", [P, BATCH * ROWPAIRS])
        counts = sb("counts", [P, 4])
        w1h, w1l = sbr("w1h", [P, KC * HIDDEN]), sbr("w1l", [P, KC * HIDDEN])
        w2h, w2l = sbr("w2h", [P, KC * HIDDEN]), sbr("w2l", [P, KC * HIDDEN])

        with ExitStack() as scope:
            def sb(name, shape):
                return scope.enter_context(nc.sbuf_tensor(name, shape, F32))

            with nc.sbuf_tensor("wraw", [P, WPART], F32) as wraw:
                pass
            xn = sb("xn", [P, UNIT])
            xs1 = sb("xs1", [P, UNIT])
            res = sb("res", [P, 2, UNIT])
            y = sb("y", [P, HALF, 2, SIDE])
            z = sb("z", [P, 2, 4 * PAIR])
            zs = sb("zs", [P, 2, 4 * PAIR])
            zf = sb("zf", [P, 2, 2, 2 * P])
            h = sb("h", [P, 2, 2, 2 * P])
            clamp = sb("clamp", [P, 4 * PAIR])
            u = sb("u", [P, 2, 2, 2 * PAIR])
            v = sb("v", [P, SIDE, 2, HALF])
            vt = sb("vt", [P, 2, CHUNK * PAIR])
            wstage = sb("wstage", [P, 2, W_COLS])
            w = sb("w", [P, 2, W_COLS])
            st = sb("st", [P, BATCH * ROWPAIRS, PAIRS, 6])
            xs = (sb("xs0", [P, UNIT]), xs1)
        with ExitStack() as scope:
            def sb(name, shape, dtype=F32):
                return scope.enter_context(nc.sbuf_tensor(name, shape, dtype))

            xm = sb("xm", [P, 2, 4, CHANNELS])
            g = sb("g", [P, 2, TOKENS])
            gl = sb("gl", [P, 4, TOKENS], F32R)
            xh = sb("xh", [P, 2, 4, CHANNELS])
            om = sb("om", [P, 2, 4, CHANNELS])
            mt = sb("mt", [P, KC, TOKENS])
            mth, mtl = sb("mth", [P, 2, KC, TOKENS], F32R), sb("mtl", [P, 2, KC, TOKENS], F32R)
            gh = sb("gh", [P, 4, TOKENS], F32R)

        ps = ctx.enter_context(nc.psum_tensor("ps", [P, 8, 512], F32))
        T_BANK, F2_BANK, T2_BANK, M1_BANK, M2_BANK, F5_BANK = range(6)
        F1_BANKS = TT_BANKS = (6, 7)
        F6_BANKS = (M2_BANK, F5_BANK)
        TURN_BANKS, MM1_BANKS, MM2_BANKS = (6, 7), (4, 5), (0, 1, 2, 3)

        s_const, s_wts = sem("s_const"), sem("s_wts")
        x_loaded = [[sem(f"x_loaded{b}{part}") for part in range(HALVES)] for b in range(BATCH)]
        stored = [sem("stored0"), sem("stored1")]
        w_loaded, w_ready = sem("w_loaded"), sem("w_ready")
        f1_done, t_done, f2_done, m1_done = sem("f1_done"), sem("t_done"), sem("f2_done"), sem("m1_done")
        m2_done, f5_done, tt_done, f6_done = sem("m2_done"), sem("f5_done"), sem("tt_done"), sem("f6_done")
        y_ready, z_ready, zf_ready, h_ready = sem("y_ready"), sem("z_ready"), sem("zf_ready"), sem("h_ready")
        clamped, u_ready, v_ready = sem("clamped"), sem("u_ready"), sem("v_ready")
        vt_ready, res_ready = sem("vt_ready"), sem("res_ready")
        t2_done, zs_ready = sem("t2_done"), sem("zs_ready")
        gcol_ready, shifted = sem("gcol_ready"), sem("shifted")
        centred, gained, ln_step, sum_ready = sem("centred"), sem("gained"), sem("ln_step"), sem("sum_ready")
        st_done, mv_ready, rs_step, rstd_ready = sem("st_done"), sem("mv_ready"), sem("rs_step"), sem("rstd_ready")
        wpart_loaded, wpart_high, wpart_low = sem("wpart_loaded"), sem("wpart_high"), sem("wpart_low")
        m_loaded = [sem("m_loaded0"), sem("m_loaded1")]
        m_stored = [sem("m_stored0"), sem("m_stored1")]
        st2_done, mv2_ready, rs2_step, rstd2_ready = sem("st2_done"), sem("mv2_ready"), sem("rs2_step"), sem("rstd2_ready")
        xh_ready, skip_ready = sem("xh_ready"), sem("skip_ready")
        turned, mt_ready, mt_high, mt_low = sem("turned"), sem("mt_ready"), sem("mt_high"), sem("mt_low")
        mm1_done, g_ready, g_high, g_low = sem("mm1_done"), sem("g_ready"), sem("g_high"), sem("g_low")
        mm2_done, om_ready = sem("mm2_done"), sem("om_ready")

        def basis(col, width=P):
            return const[:, col:col + width]

        def wpart(first, second, n):
            m = n % WPARTS
            return (first if n < WPARTS else second)[:, m * WPART:(m + 1) * WPART]

        ident = basis(C_ID)
        SPLIT_AT = 2
        TURN_AT = 8

        def unit_view(a, b, i):
            return a[b].rearrange("(r p) c -> p r c", p=P)[:, :, bass.ds(i * PAIR, PAIR)]

        def half_view(a, b, i, part):
            n = ROWPAIRS // HALVES
            return unit_view(a, b, i)[:, part * n:(part + 1) * n]

        def half_buffer(t, part):
            n = UNIT // HALVES
            return t[:, part * n:(part + 1) * n].rearrange("p (r c) -> p r c", c=PAIR)

        def tile_view(a, n):
            return a.rearrange("b (n j p) c -> p (b n) j c", p=P, j=4)[:, bass.ds(n, 1)].rearrange("p o j c -> p (o j) c")

        block = ctx.enter_context(nc.Block())

        @block.sync
        def _(sp):
            sp.dma_start(const[:, :], consts).then_inc(s_const, 16)

            def load_weights(L, i):
                sp.dma_start(wstage[0:ROWS, :, :],
                             spectral[L.index].rearrange("(g k) p n -> p g k n", k=2)[:, bass.ds(i, 1)]
                             .rearrange("p o k n -> p (o k) n")).then_inc(w_loaded, 16)

            def load_half(L, b, i, part):
                sp.dma_start(half_buffer(xs[b], part),
                             half_view(layer_in[L.index], b, i, part)).then_inc(x_loaded[b][part], 16)

            def spectral_layer(L, loaded, following):
                if not loaded:
                    for part in range(HALVES):
                        load_half(L, 0, 0, part)
                    load_weights(L, 0)
                    for part in range(HALVES):
                        load_half(L, 1, 0, part)
                if L.index == 0:
                    split_loads()

                def body(i, last):
                    if not last or following:
                        sp.wait_ge(w_ready, 5 * (PAIRS * L.index + 1) + i * 5)
                        load_weights(following if last else L, 0 if last else i + 1)
                    for b in range(BATCH):
                        if L.index == 1 and last and b == 1:
                            sp.wait_ge(stored[0], 32 * PAIRS * (L.index + 1))
                            sp.wait_ge(gained, 2 * PAIRS)
                            sp.wait_ge(f1_done, CHUNKS * layers[2].units)
                            for r in range(2):
                                sp.dma_start(xm[:, r], tile_view(after[1], r)).then_inc(m_loaded[r], 16)
                        for part in range(HALVES):
                            sp.wait_ge(res_ready, CHUNKS * (L.units + b) + HALF_CHUNKS * (part + 1) + i * (2 * CHUNKS))
                            sp.dma_start(half_view(layer_out[L.index], b, i, part),
                                         half_buffer(res[:, b], part)).then_inc(stored[b], 16)
                            if not last:
                                load_half(L, b, i + 1, part)
                            elif following:
                                sp.wait_ge(stored[b], 32 * (PAIRS * L.index + 1))
                                load_half(following, b, 0, part)

                iterate(sp, PAIRS, body)

            def split_loads():
                for n in range(2 * WPARTS):
                    if n:
                        sp.wait_ge(wpart_low, n)
                    m = n % WPARTS
                    if n < WPARTS:
                        src = w1[m // 2 * P:(m // 2 + 1) * P, m % 2 * WPART:(m % 2 + 1) * WPART]
                    else:
                        src = w2[2 * m * P:2 * (m + 1) * P, :].rearrange("(k p) n -> p k n", p=P)
                    dst = wraw[:, :] if n < WPARTS else wraw[:, :].rearrange("p (k n) -> p k n", k=2)
                    sp.dma_start(dst, src).then_inc(wpart_loaded, 16)
                sp.dma_start(lnrow[:, :, :], ln1.rearrange("a c -> (a c)").partition_broadcast(P)
                             .rearrange("p (a c) -> p a c", a=2)).then_inc(s_wts, 16)
                sp.dma_start(lncol[0:PAIR, :, :], lncol_in).then_inc(s_wts, 16)
                sp.dma_start(b2row[:, :], b2.partition_broadcast(P)).then_inc(s_wts, 16)
                sp.dma_start(colp[:, :], cols).then_inc(s_wts, 16)

            def token_mlp_moves():
                sp.wait_ge(stored[1], 32 * PAIRS * 2)

                def body(i, last):
                    for r in range(2):
                        if last and r == 1:
                            for n in range(2):
                                sp.wait_ge(m_stored[n], 16 * TILES // (2 * BATCH))
                            for part in range(HALVES):
                                load_half(layers[2], 0, 0, part)
                            load_weights(layers[2], 0)
                        sp.wait_ge(om_ready, 4 * (r + 1) + i * 8)
                        sp.dma_start(tile_view(after[2], 2 * i + r), om[:, r]).then_inc(m_stored[r], 16)
                        if not last:
                            sp.dma_start(xm[:, r], tile_view(after[1], 2 * i + (2 + r))).then_inc(m_loaded[r], 16)

                iterate(sp, TILES // 2, body)
                for r in range(2):
                    sp.wait_ge(m_stored[r], 16 * TILES // 2)
                for part in range(HALVES):
                    load_half(layers[2], 1, 0, part)

            spectral_layer(layers[0], False, layers[1])
            spectral_layer(layers[1], True, None)
            token_mlp_moves()
            spectral_layer(layers[2], True, layers[3])
            spectral_layer(layers[3], True, None)
            for b in range(BATCH):
                sp.wait_ge(stored[b], 32 * PAIRS * 4)

        @block.tensor
        def _(pe):
            pe.wait_ge(s_const, 16)
            def f1(L, b, i, k):
                if L.norm:
                    pe.wait_ge(centred, CHUNKS * b + k + 1 + i * (2 * CHUNKS))
                    src = xn
                else:
                    if k % HALF_CHUNKS == 0:
                        pe.wait_ge(x_loaded[b][k // HALF_CHUNKS], 16 * (PAIRS * L.index + 1) + i * 16)
                    src = xs[b]
                if k >= 2:
                    pe.wait_ge(y_ready, CHUNKS * (L.units + b) + k - 1 + i * (2 * CHUNKS))
                for j in range(CHUNK):
                    r = CHUNK * k + j
                    mm = pe.matmul(ps[0:PAIR, F1_BANKS[k % 2], j * P:(j + 1) * P],
                                   src[:, r * PAIR:(r + 1) * PAIR], basis(C_D1), start=True, stop=True)
                mm.then_inc(f1_done, 1)

            def post(L, b, i, t, beside):
                base = CHUNKS * (L.units + b)
                if t == 0:
                    pe.wait_ge(v_ready, L.chain + (b + 1) * L.n + i * (2 * L.n))
                    if beside:
                        pe.wait_ge(y_ready, base + 2 * CHUNKS - 1 + i * (2 * CHUNKS))
                if t < CHUNKS:
                    for j in range(CHUNK):
                        r = 2 * (CHUNK * t + j)
                        mm = pe.transpose(ps[:, TT_BANKS[t % 2], j * PAIR:(j + 1) * PAIR],
                                          v[0:PAIR, r:r + 2].rearrange("p a b c -> p (a b c)"),
                                          ident[0:PAIR, 0:PAIR])
                    mm.then_inc(tt_done, 1)
                k = t - 1
                if k >= 0:
                    pe.wait_ge(vt_ready, base + k + 1 + i * (2 * CHUNKS))
                    if k >= 2:
                        pe.wait_ge(res_ready, base + k - 1 + i * (2 * CHUNKS))
                    pe.matmul(ps[:, F6_BANKS[k % 2], 0:CHUNK * PAIR], basis(C_D6), vt[:, k % 2, :],
                              start=True, stop=True).then_inc(f6_done, 1)

            def turn(r, i, k):
                if k == 0:
                    pe.wait_ge(xh_ready, 4 * (r + 1) + i * 8)
                if k >= 2:
                    pe.wait_ge(mt_ready, KC * r + k - 1 + i * (2 * KC))
                for j in range(4):
                    mm = pe.transpose(ps[:, TURN_BANKS[k % 2], j * P:(j + 1) * P],
                                      xh[:, r, j, k * P:(k + 1) * P], ident)
                mm.then_inc(turned, 1)

            def chain(L, b, i, before, after):
                done = L.chain + b * L.n
                step = 2 * L.n
                if before:
                    post(*before, 0, True)
                for t in range(L.n + STAGES - 1):
                    k = t - 5
                    if 0 <= k < L.n:
                        pe.wait_ge(u_ready, done + k + 1 + i * step)
                        if k >= 1:
                            pe.wait_ge(v_ready, done + k + i * step)
                        for half, pos, col, width, to, first, final in L.groups[k][4]:
                            mm = pe.matmul(ps[0:PAIR, F5_BANK, to:to + width],
                                           u[:, k % 2, half, pos * PAIR:(pos + 1) * PAIR],
                                           basis(col, width), start=first, stop=final)
                        mm.then_inc(f5_done, 1)
                    k = t - 4
                    if 0 <= k < L.n:
                        pe.wait_ge(h_ready, 2 * (done + k + 1) + i * (2 * step))
                        if k == 0 and before:
                            pb = before
                            pe.wait_ge(res_ready, CHUNKS * (pb[0].units + pb[1] + 1) + pb[2] * (2 * CHUNKS))
                        npos = L.groups[k][2]
                        to = ps[:, M2_BANK, 0:npos * 2 * PAIR].rearrange("p (a q n c) -> p a q n c", a=2, q=npos, n=2)
                        for pos in range(npos):
                            for n in range(2):
                                mm = pe.matmul(to[:, :, pos, n], h[0:ROWS, k % 2, n, pos * P:(pos + 1) * P],
                                               w[0:ROWS, n, SECOND:BIAS].rearrange("p (a c) -> p a c", a=2),
                                               start=True, stop=True)
                        mm.then_inc(m2_done, 1)
                    k = t - 3
                    if 0 <= k < L.n:
                        pe.wait_ge(zf_ready, done + k + 1 + i * step)
                        if k == 0 and b == 0:
                            pe.wait_ge(w_ready, 5 * (PAIRS * L.index + 1) + i * 5)
                        width = L.groups[k][2] * P
                        for n in range(2):
                            mm = pe.matmul(ps[0:ROWS, M1_BANK, n * 2 * P:n * 2 * P + width], w[0:PAIR, n, 0:ROWS],
                                           zf[0:PAIR, k % 2, n, 0:width], start=True, stop=True)
                        mm.then_inc(m1_done, 1)
                    k = t - 2
                    if 0 <= k < L.n:
                        pe.wait_ge(zs_ready, done + k + 1 + i * step)
                        for pos in range(L.groups[k][2]):
                            for n in range(2):
                                at, to = (2 * pos + n) * PAIR, (2 * n + pos) * P
                                mm = pe.transpose(ps[0:PAIR, T2_BANK, to:to + P], zs[:, k % 2, at:at + PAIR], ident)
                        mm.then_inc(t2_done, 1)
                    k = t - 1
                    if 0 <= k < L.n:
                        pe.wait_ge(z_ready, done + k + 1 + i * step)
                        npos = L.groups[k][2]
                        to = ps[:, F2_BANK, 0:npos * 2 * PAIR].rearrange("p (q n a c) -> p q n a c", q=npos, n=2, a=2)
                        src = z[:, k % 2, :].rearrange("p (s n c) -> p s n c", n=2, c=BLOCK)
                        for ri in range(2):
                            for p0, rows, col, slots in L.groups[k][3]:
                                stop = slots[-1] + 1
                                by = slots[1] - slots[0] if len(slots) > 1 else 1
                                mm = pe.matmul(to[p0:p0 + rows, :, :, ri], basis(col + ri * SIDE, rows),
                                               src[:, slots[0]:stop:by], start=True, stop=True)
                        mm.then_inc(f2_done, 1)
                    k = t
                    if k < L.n:
                        if k == 0:
                            if L.norm:
                                pe.wait_ge(shifted, b + 1 + i * 2)
                            else:
                                pe.wait_ge(y_ready, CHUNKS * (L.units + b + 1) + i * (2 * CHUNKS))
                        s0, slots = L.groups[k][0:2]
                        for j in range(slots):
                            mm = pe.transpose(ps[:, T_BANK, j * PAIR:(j + 1) * PAIR],
                                              y[0:PAIR, s0 + j].rearrange("p a b -> p (a b)"),
                                              ident[0:PAIR, 0:PAIR])
                        mm.then_inc(t_done, 1)
                    if before and t < len(POST_BESIDE):
                        for p in POST_BESIDE[t]:
                            post(*before, p, True)
                    if after and t >= L.n:
                        for p in F1_BESIDE[t - L.n]:
                            f1(*after, p)
                    if L.norm and not after and 0 <= t - L.n - 1 < KC:
                        turn(0, 0, t - L.n - 1)

            def spectral_layer(L, previous, following):
                if not previous:
                    for k in range(CHUNKS):
                        f1(L, 0, 0, k)
                    if L.index > 0:
                        pe.wait_ge(om_ready, 4 * TILES)

                def body(i, last):
                    before = (previous, 1, PAIRS - 1) if first_of(i) else (L, 1, i - 1)
                    after = (L, 0, i + 1) if not last else (following, 0, 0)
                    chain(L, 0, i, before if before[0] else None, (L, 1, i))
                    chain(L, 1, i, (L, 0, i), after if after[0] else None)

                iterate(pe, PAIRS, body)
                if not following:
                    for t in range(CHUNKS + 1):
                        post(L, 1, PAIRS - 1, t, False)

            def token_mlp():
                def first(r, i, n):
                    if n == 0:
                        pe.wait_ge(mt_low, KC * (r + 1) + i * (2 * KC))
                    if n >= 2:
                        pe.wait_ge(g_ready, HC * r + n - 1 + i * (2 * HC))
                    for k in range(KC):
                        at = slice(k * HIDDEN + n * P, k * HIDDEN + (n + 1) * P)
                        for m, (a, b) in enumerate([(w1h, mth), (w1h, mtl), (w1l, mth)]):
                            mm = pe.matmul(ps[:, MM1_BANKS[n % 2], :], a[:, at], b[:, r, k, :],
                                           start=k == 0 and m == 0, stop=k == KC - 1 and m == 2)
                    mm.then_inc(mm1_done, 1)

                def second(r, i, n):
                    pe.wait_ge(g_low, HC * r + n + 1 + i * (2 * HC))
                    if n == 0:
                        wait_past(pe, om_ready, 4 * r + i * 8)
                    at = slice(n * CHANNELS, (n + 1) * CHANNELS)
                    for j in range(4):
                        part = slice(j * P, (j + 1) * P)
                        for m, (a, b) in enumerate([(gh, w2h), (gh, w2l), (gl, w2h)]):
                            mm = pe.matmul(ps[:, MM2_BANKS[j], 0:CHANNELS], a[:, n % 4, part], b[:, at],
                                           start=n == 0 and m == 0, stop=n == HC - 1 and m == 2)
                        if n == HC - 1:
                            mm.then_inc(mm2_done, 1)

                def tile(r, i, following):
                    for t in range(HC + LAG):
                        if t < HC:
                            first(r, i, t)
                        if 0 <= t - TURN_AT < KC and following:
                            turn(*following, t - TURN_AT)
                        if t >= LAG:
                            second(r, i, t - LAG)

                def body(i, last):
                    tile(0, i, (1, i))
                    tile(1, i, None if last else (0, i + 1))

                pe.wait_ge(res_ready, CHUNKS * layers[2].units)
                iterate(pe, TILES // 2, body)

            spectral_layer(layers[0], None, layers[1])
            spectral_layer(layers[1], layers[0], None)
            token_mlp()
            spectral_layer(layers[2], None, layers[3])
            spectral_layer(layers[3], layers[2], None)

        @block.scalar
        def _(act):
            def f1(L, b, i, k):
                act.wait_ge(f1_done, CHUNKS * (L.units + b) + k + 1 + i * (2 * CHUNKS))
                r = 2 * CHUNK * k
                to = y[0:PAIR].rearrange("p k a r -> p r a k")[:, r:r + 2 * CHUNK]
                src = ps[0:PAIR, F1_BANKS[k % 2], :].rearrange("p (r a k) -> p r a k", a=2, k=HALF)
                if not L.norm:
                    act.activation(to, src, ACT.Copy).then_inc(y_ready, 1)
                    return
                if k == 0 and b == 0:
                    act.wait_ge(gcol_ready, 1 + i)
                act.activation(to, src, ACT.Identity, scale=gcol[0:PAIR, 0:1]).then_inc(y_ready, 1)
                if k == CHUNKS - 1:
                    act.wait_ge(y_ready, CHUNKS * (L.units + b + 1) + i * (2 * CHUNKS))
                    act.activation(y[0:PAIR, 0, 0, :], y[0:PAIR, 0, 0, :], ACT.Identity,
                                   bias=gcol[0:PAIR, 1:2]).then_inc(shifted, 1)

            def post(L, b, i, t):
                if t < CHUNKS:
                    act.wait_ge(tt_done, CHUNKS * (L.units + b) + t + 1 + i * (2 * CHUNKS))
                    act.activation(vt[:, t % 2, :], ps[:, TT_BANKS[t % 2], 0:CHUNK * PAIR],
                                   ACT.Copy).then_inc(vt_ready, 1)

            def turn(r, i, k):
                act.wait_ge(turned, KC * r + k + 1 + i * (2 * KC))
                act.activation(mt[:, k, :], ps[:, TURN_BANKS[k % 2], :], ACT.Identity,
                               scale=colp[:, HC + k:HC + k + 1],
                               bias=colp[:, HC + KC + k:HC + KC + k + 1]).then_inc(mt_ready, 1)

            def chain(L, b, i, before, after):
                done = L.chain + b * L.n
                step = 2 * L.n
                if before:
                    post(*before, 0)
                for t in range(L.n + STAGES - 1):
                    k = t - 5
                    if 0 <= k < L.n:
                        act.wait_ge(f5_done, done + k + 1 + i * step)
                        s0, slots = L.groups[k][0:2]
                        act.activation(v[0:PAIR].rearrange("p r a k -> p k a r")[:, s0:s0 + slots],
                                       ps[0:PAIR, F5_BANK, 0:slots * P].rearrange("p (k a r) -> p k a r", a=2, r=SIDE),
                                       ACT.Copy, scale=L.inverse).then_inc(v_ready, 1)
                    k = t - 3
                    if 0 <= k < L.n:
                        act.wait_ge(m1_done, done + k + 1 + i * step)
                        width = L.groups[k][2] * P
                        for n in range(2):
                            act.activation(h[0:ROWS, k % 2, n, 0:width],
                                           ps[0:ROWS, M1_BANK, n * 2 * P:n * 2 * P + width],
                                           L.act, bias=w[0:ROWS, n, BIAS:W_COLS]).then_inc(h_ready, 1)
                    k = t - 2
                    if 0 <= k < L.n:
                        act.wait_ge(t2_done, done + k + 1 + i * step)
                        width = L.groups[k][2] * P
                        act.activation(zf[0:PAIR, k % 2, :, 0:width],
                                       ps[0:PAIR, T2_BANK, :].rearrange("p (n m) -> p n m", n=2)[:, :, 0:width],
                                       ACT.Copy).then_inc(zf_ready, 1)
                    k = t
                    if k < L.n:
                        act.wait_ge(t_done, done + k + 1 + i * step)
                        n = L.groups[k][1] * PAIR
                        act.activation(z[:, k % 2, 0:n], ps[:, T_BANK, 0:n], ACT.Copy).then_inc(z_ready, 1)
                    if before and t < len(POST_BESIDE):
                        for p in POST_BESIDE[t]:
                            post(*before, p)
                    if after and t >= L.n:
                        for p in F1_BESIDE[t - L.n]:
                            f1(*after, p)
                    if L.norm and not after and 0 <= t - L.n - 1 < KC:
                        if t == L.n + 1:
                            act.wait_ge(s_wts, 64)
                        turn(0, 0, t - L.n - 1)
                    if L.index == 0 and b == 0 and first_of(i) and 0 <= t - SPLIT_AT < 2 * WPARTS:
                        act.wait_ge(wpart_loaded, 16 * (t - SPLIT_AT + 1))
                        act.activation(wpart(w1h, w2h, t - SPLIT_AT), wraw[:, :], ACT.Copy).then_inc(wpart_high, 1)

            def spectral_layer(L, previous, following):
                if not previous:
                    for k in range(CHUNKS):
                        f1(L, 0, 0, k)

                def body(i, last):
                    before = (previous, 1, PAIRS - 1) if first_of(i) else (L, 1, i - 1)
                    after = (L, 0, i + 1) if not last else (following, 0, 0)
                    chain(L, 0, i, before if before[0] else None, (L, 1, i))
                    chain(L, 1, i, (L, 0, i), after if after[0] else None)

                iterate(act, PAIRS, body)
                if not following:
                    for t in range(CHUNKS + 1):
                        post(L, 1, PAIRS - 1, t)

            def token_mlp():
                def first(r, i, n):
                    act.wait_ge(mm1_done, HC * r + n + 1 + i * (2 * HC))
                    wait_past(act, g_low, HC * r + n - 1 + i * (2 * HC))
                    act.activation(g[:, n % 2, :], ps[:, MM1_BANKS[n % 2], :], ACT.Gelu,
                                   bias=colp[:, n:n + 1]).then_inc(g_ready, 1)
                    act.wait_ge(g_ready, HC * r + n + 1 + i * (2 * HC))
                    act.activation(gh[:, n % 4, :], g[:, n % 2, :], ACT.Copy).then_inc(g_high, 1)

                def tile(r, i, following):
                    for t in range(HC):
                        first(r, i, t)
                        if 0 <= t - TURN_AT < KC and following:
                            turn(*following, t - TURN_AT)

                def body(i, last):
                    tile(0, i, (1, i))
                    tile(1, i, None if last else (0, i + 1))

                act.wait_ge(res_ready, CHUNKS * layers[2].units)
                iterate(act, TILES // 2, body)

            spectral_layer(layers[0], None, layers[1])
            spectral_layer(layers[1], layers[0], None)
            token_mlp()
            spectral_layer(layers[2], None, layers[3])
            spectral_layer(layers[3], layers[2], None)

        @block.vector
        def _(dve):
            def chain(L, b, i, before, extra):
                done = L.chain + b * L.n
                step = 2 * L.n
                shrunk = done if L.index == 0 else done - 2 * PAIRS * layers[1].n
                if before:
                    post(*before, 0)
                for t in range(L.n + STAGES - 1):
                    k = t - 4
                    if 0 <= k < L.n:
                        dve.wait_ge(m2_done, done + k + 1 + i * step)
                        n = L.groups[k][2] * PAIR
                        if L.shrink:
                            dve.tensor_scalar(clamp[:, 0:2 * n], ps[:, M2_BANK, 0:2 * n], LAMBDA, -LAMBDA,
                                              ALU.min, ALU.max).then_inc(clamped, 1)
                            dve.wait_ge(clamped, shrunk + k + 1 + i * step)
                        for half in range(2):
                            rows = slice(half * SIDE, (half + 1) * SIDE)
                            for ri in range(2):
                                at = slice(ri * n, (ri + 1) * n)
                                to = u[ri * SIDE:(ri + 1) * SIDE, k % 2, half, 0:n]
                                if L.shrink:
                                    ins = dve.tensor_tensor(to, ps[rows, M2_BANK, at], clamp[rows, at], ALU.subtract)
                                else:
                                    ins = dve.tensor_copy(to, ps[rows, M2_BANK, at])
                        ins.then_inc(u_ready, 1)
                    k = t - 1
                    if 0 <= k < L.n:
                        dve.wait_ge(f2_done, done + k + 1 + i * step)
                        n = L.groups[k][2] * 2 * PAIR
                        dve.tensor_scalar(zs[:, k % 2, 0:n], ps[:, F2_BANK, 0:n],
                                          L.forward, None, ALU.mult).then_inc(zs_ready, 1)
                    if before and t < len(POST_BESIDE):
                        for p in POST_BESIDE[t]:
                            post(*before, p)
                    for work in extra.get(t, ()):
                        work()

            def split(n):
                dve.wait_ge(wpart_high, n + 1)
                dve.tensor_tensor(wpart(w1l, w2l, n), wraw[:, :], wpart(w1h, w2h, n),
                                  ALU.subtract).then_inc(wpart_low, 1)

            def aggregate(b, part):
                n = ROWPAIRS // HALVES
                dve.wait_ge(st_done, (2 * PAIRS - 1 + b) * ROWPAIRS)
                for r in range(b * ROWPAIRS + part * n, b * ROWPAIRS + (part + 1) * n):
                    dve.bn_aggr(mv[:, r, :], st[:, r].rearrange("p a b -> p (a b)")).then_inc(mv_ready, 1)

            def centre(b, i, k):
                if k % HALF_CHUNKS == 0:
                    dve.wait_ge(x_loaded[b][k // HALF_CHUNKS], 16 * (PAIRS + 1) + i * 16)
                if k == 0:
                    if first_of(i):
                        dve.wait_ge(mv_ready, (b + 1) * ROWPAIRS)
                        dve.wait_ge(rstd_ready, b + 1)
                    if b == 1 or not first_of(i):
                        dve.wait_ge(f1_done, CHUNKS * (layers[1].units + b) + i * (2 * CHUNKS))
                        dve.wait_ge(gained, b + i * 2)
                for r in range(k * CHUNK, (k + 1) * CHUNK):
                    at, row = slice(r * PAIR, (r + 1) * PAIR), b * ROWPAIRS + r
                    ins = dve.tensor_scalar(xn[:, at], xs[b][:, at], mv[:, row, 0:1], rstd[:, row:row + 1],
                                            ALU.subtract, ALU.mult)
                ins.then_inc(centred, 1)

            def post(L, b, i, t):
                base = CHUNKS * (L.units + b)
                k = t - 1
                if k == 0:
                    if L.norm:
                        dve.wait_ge(sum_ready, b + 1 + i * 2)
                    else:
                        for part in range(HALVES):
                            dve.wait_ge(x_loaded[b][part], 16 * (PAIRS * L.index + 1) + i * 16)
                    if not (L.index == 0 and first_of(i)):
                        dve.wait_ge(stored[b], 32 * PAIRS * L.index + i * 32)
                if k >= 0:
                    dve.wait_ge(f6_done, base + k + 1 + i * (2 * CHUNKS))
                    at = slice(k * CHUNK * PAIR, (k + 1) * CHUNK * PAIR)
                    dve.tensor_tensor(res[:, b, at], ps[:, F6_BANKS[k % 2], 0:CHUNK * PAIR], xs[b][:, at],
                                      ALU.add).then_inc(res_ready, 1)
                    if L.index == 0:
                        dve.wait_ge(res_ready, base + k + 1 + i * (2 * CHUNKS))
                        for r in range(k * CHUNK, (k + 1) * CHUNK):
                            dve.bn_stats(st[:, b * ROWPAIRS + r, i if isinstance(i, int) else bass.ds(i, 1), :],
                                         res[:, b, r * PAIR:(r + 1) * PAIR]).then_inc(st_done, 1)

            def statistics(r, i):
                dve.wait_ge(m_loaded[r], 16 + i * 16)
                for j in range(4):
                    dve.bn_stats(stat[:, r, j, :], xm[:, r, j, :]).then_inc(st2_done, 1)
                dve.wait_ge(st2_done, 4 * (r + 1) + i * 8)
                dve.tensor_copy(counts[:, :], stat[:, r, :, 0])
                for j in range(4):
                    dve.bn_aggr(mv2[:, r, j, :], stat[:, r, j, :]).then_inc(mv2_ready, 1)

            def normalise(r, i):
                dve.wait_ge(mv2_ready, 4 * (r + 1) + i * 8)
                dve.wait_ge(rstd2_ready, r + 1 + i * 2)
                for j in range(4):
                    dve.tensor_scalar(xh[:, r, j, :], xm[:, r, j, :], mv2[:, r, j, 0:1], rstd2[:, r, j:j + 1],
                                      ALU.subtract, ALU.mult).then_inc(xh_ready, 1)

            def split_input(r, i, k):
                dve.wait_ge(mt_ready, KC * r + k + 1 + i * (2 * KC))
                dve.tensor_copy(mth[:, r, k, :], mt[:, k, :]).then_inc(mt_high, 1)
                dve.wait_ge(mt_high, KC * r + k + 1 + i * (2 * KC))
                dve.tensor_tensor(mtl[:, r, k, :], mt[:, k, :], mth[:, r, k, :],
                                  ALU.subtract).then_inc(mt_low, 1)

            def spectral_layer(L, previous, following):
                def centre_steps(b, i):
                    return {L.n - 2 + n: [lambda n=n: (centre(b, i, 2 * n), centre(b, i, 2 * n + 1))]
                            for n in range(CHUNKS // 2)}

                def body(i, last):
                    first, second = {}, {}
                    if L.index == 0 and first_of(i):
                        first = {SPLIT_AT + t: [lambda t=t: split(t)] for t in range(2 * WPARTS)}
                    if L.norm:
                        first = centre_steps(1, i)
                        if first_of(i):
                            first.update({3 + part: [lambda part=part: aggregate(1, part)] for part in range(HALVES)})
                        if not last:
                            second = centre_steps(0, i + 1)
                        else:
                            second = {L.n - 2: [lambda: statistics(0, 0)], L.n: [lambda: normalise(0, 0)]}
                    if L.index == 0 and last:
                        second = centre_steps(0, 0)
                        second.update({4 + part: [lambda part=part: aggregate(0, part)] for part in range(HALVES)})
                    before = (previous, 1, PAIRS - 1) if first_of(i) else (L, 1, i - 1)
                    chain(L, 0, i, before if before[0] else None, first)
                    chain(L, 1, i, (L, 0, i), second)

                iterate(dve, PAIRS, body)
                if not following:
                    for t in range(CHUNKS + 1):
                        post(L, 1, PAIRS - 1, t)
                        if L.norm and t < KC:
                            split_input(0, 0, t)

            def token_mlp():
                def split_hidden(r, i, n):
                    dve.wait_ge(g_high, HC * r + n + 1 + i * (2 * HC))
                    dve.tensor_tensor(gl[:, n % 4, :], g[:, n % 2, :], gh[:, n % 4, :],
                                      ALU.subtract).then_inc(g_low, 1)

                def results(r, i):
                    if r == 0 and first_of(i):
                        dve.wait_ge(stored[1], 32 * PAIRS * 2)
                    dve.wait_ge(skip_ready, r + 1 + i * 2)
                    wait_past(dve, m_stored[r], i * 16)
                    for j in range(4):
                        dve.wait_ge(mm2_done, 4 * r + j + 1 + i * 8)
                        dve.tensor_tensor(om[:, r, j, :], ps[:, MM2_BANKS[j], 0:CHANNELS], xm[:, r, j, :],
                                          ALU.add).then_inc(om_ready, 1)

                def tile(r, i, following):
                    for t in range(HC):
                        split_hidden(r, i, t)
                        if following:
                            if t == TURN_AT - 5:
                                statistics(*following)
                            if t == TURN_AT - 3:
                                normalise(*following)
                            if 0 <= t - TURN_AT < KC:
                                split_input(*following, t - TURN_AT)
                    results(r, i)

                def body(i, last):
                    tile(0, i, (1, i))
                    tile(1, i, None if last else (0, i + 1))

                iterate(dve, TILES // 2, body)

            spectral_layer(layers[0], None, layers[1])
            spectral_layer(layers[1], layers[0], None)
            token_mlp()
            spectral_layer(layers[2], None, layers[3])
            spectral_layer(layers[3], layers[2], None)

        @block.gpsimd
        def _(pool):
            pool.memset(power[:, :], -0.5).then_inc(rs_step, 1)
            pool.memset(eps[:, :], LN_EPS).then_inc(rs_step, 1)
            pool.wait_ge(s_const, 16)

            def weights(L, i):
                pool.wait_ge(w_loaded, 16 * (PAIRS * L.index + 1) + i * 16)
                wait_past(pool, m2_done, L.chain + i * (2 * L.n))
                real = C_SIGN + (1 if L.act == ACT.Gelu else 0)
                imag = SECOND + BLOCK
                src, to = wstage[0:ROWS], w[0:ROWS]
                pool.tensor_tensor(to[:, :, 0:BLOCK], src[:, :, 0:BLOCK],
                                   const[0:ROWS, C_SIGN:C_SIGN + 1].unsqueeze(1).to_broadcast([ROWS, 2, BLOCK]),
                                   ALU.mult).then_inc(w_ready, 1)
                pool.tensor_copy(to[:, :, BLOCK:ROWS], src[:, :, BLOCK:ROWS]).then_inc(w_ready, 1)
                pool.tensor_scalar(to[:, :, SECOND:imag], src[:, :, SECOND:imag], const[0:ROWS, real:real + 1], None,
                                   ALU.mult).then_inc(w_ready, 1)
                if L.act == ACT.Gelu:
                    pool.tensor_scalar(to[:, :, imag:BIAS], src[:, :, imag:BIAS],
                                       const[0:ROWS, C_SIGN + 2:C_SIGN + 3], None, ALU.mult).then_inc(w_ready, 1)
                else:
                    pool.tensor_copy(to[:, :, imag:BIAS], src[:, :, imag:BIAS]).then_inc(w_ready, 1)
                pool.tensor_copy(to[:, :, BIAS:], src[:, :, BIAS:]).then_inc(w_ready, 1)

            def norm_columns(i):
                if not first_of(i):
                    pool.wait_ge(shifted, i * 2)
                pool.tensor_tensor(gcol[0:PAIR, :], lncol[0:PAIR, bass.ds(i, 1), :].rearrange("p o a -> p (o a)"),
                                   const[0:PAIR, C_SIGN + 3:C_SIGN + 5], ALU.mult).then_inc(gcol_ready, 1)

            def gain(b, i):
                xo = xn[:, :].rearrange("p (r c) -> p r c", c=PAIR)
                rv = res[:, b, :].rearrange("p (r c) -> p r c", c=PAIR)
                gain = lnrow[:, 0:1, bass.ds(i * PAIR, PAIR)].to_broadcast([P, ROWPAIRS, PAIR])
                pool.wait_ge(centred, CHUNKS * (b + 1) + i * (2 * CHUNKS))
                pool.wait_ge(stored[b], 32 * PAIRS + i * 32)
                pool.tensor_tensor(rv, xo, gain, ALU.mult).then_inc(gained, 1)

            def residual(b, i):
                xv = xs[b][:, :].rearrange("p (r c) -> p r c", c=PAIR)
                rv = res[:, b, :].rearrange("p (r c) -> p r c", c=PAIR)
                shift = lnrow[:, 1:2, bass.ds(i * PAIR, PAIR)].to_broadcast([P, ROWPAIRS, PAIR])
                pool.wait_ge(gained, b + 1 + i * 2)
                pool.tensor_tensor(xv, xv, rv, ALU.add).then_inc(ln_step, 1)
                pool.wait_ge(ln_step, b + 1 + i * 2)
                pool.tensor_tensor(xv, xv, shift, ALU.add).then_inc(sum_ready, 1)

            def spectral_layer(L, previous, following):
                def body(i, last):
                    if L.norm:
                        gain(1, i)
                        residual(1, i)
                    if not last:
                        if L.norm:
                            norm_columns(i + 1)
                        weights(L, i + 1)
                        if L.norm:
                            gain(0, i + 1)
                            residual(0, i + 1)
                    elif following:
                        if following.norm:
                            pool.wait_ge(s_wts, 64)
                            norm_columns(0)
                            root(0)
                        weights(following, 0)
                        if following.norm:
                            gain(0, 0)
                            root(1)
                            residual(0, 0)

                if not previous:
                    weights(L, 0)
                iterate(pool, PAIRS, body)

            def root(b):
                at = slice(b * ROWPAIRS, (b + 1) * ROWPAIRS)
                pool.wait_ge(mv_ready, (b + 1) * ROWPAIRS)
                pool.tensor_tensor(rstd[:, at], mv[:, at, 1], eps[:, at], ALU.add).then_inc(rs_step, 1)
                pool.wait_ge(rs_step, 3 + b)
                pool.tensor_tensor(rstd[:, at], rstd[:, at], power[:, at], ALU.pow).then_inc(rstd_ready, 1)

            def token_mlp():
                def root2(r, i):
                    pool.wait_ge(mv2_ready, 4 * (r + 1) + i * 8)
                    pool.tensor_tensor(rstd2[:, r, :], mv2[:, r, :, 1], eps[:, 0:4], ALU.add).then_inc(rs2_step, 1)
                    pool.wait_ge(rs2_step, r + 1 + i * 2)
                    pool.tensor_tensor(rstd2[:, r, :], rstd2[:, r, :], power[:, 0:4], ALU.pow).then_inc(rstd2_ready, 1)
                    pool.wait_ge(xh_ready, 4 * (r + 1) + i * 8)
                    pool.tensor_tensor(xm[:, r], xm[:, r], b2row[:, :].unsqueeze(1).to_broadcast([P, 4, CHANNELS]),
                                       ALU.add).then_inc(skip_ready, 1)

                with pool.Fori(0, TILES // 2) as i:
                    root2(0, i)
                    root2(1, i)

            spectral_layer(layers[0], None, layers[1])
            spectral_layer(layers[1], layers[0], None)
            token_mlp()
            spectral_layer(layers[2], None, layers[3])
            spectral_layer(layers[3], layers[2], None)


def host_constants():
    import numpy as np
    n, f = np.arange(SIDE), 2 * np.pi / SIDE
    half = np.arange(HALF)
    col = np.stack([np.cos(f * np.outer(n, half)), -np.sin(f * np.outer(n, half))], 1)
    col[:, 1, 0] = (-1.0) ** n
    d1 = np.kron(np.eye(2), col.reshape(SIDE, SIDE))
    inv = 2 * col.transpose(1, 2, 0)
    inv[:, 0] /= 2
    d6 = np.kron(np.eye(2), inv.reshape(SIDE, SIDE))
    c, s = np.cos(f * np.outer(n, n)), np.sin(f * np.outer(n, n))
    o = np.zeros((SIDE, SIDE))
    d2 = np.block([[c, -s], [s, c]])
    d2a, d2b = np.block([[c, -s], [o, o]]), np.block([[o, o], [c, -s]])
    d5 = np.block([[c, s], [-s, c]])
    d5a, d5b = np.block([[c, o], [-s, o]]), np.block([[o, c], [o, -s]])

    def pair(first):
        m = np.zeros((2, 2, HALF, 2, 2 * SIDE))
        for slot, d in enumerate((first, d5)):
            m[:, slot, :, slot, :] = d.reshape(2, SIDE, 2 * SIDE)[:, :HALF]
        return m.reshape(P, 4 * SIDE)

    sign = np.ones((P, 5))
    sign[BLOCK:PAIR, 0:2] = -1
    sign[ONE_ROW, 1:3] = 1 / ONE_GELU
    sign[:, 4] = SIDE
    return np.concatenate([d1, np.eye(P), d2, d2a, d2b, d5, d5a, d5b, d6, pair(d5), pair(d5a), sign],
                          1).astype(np.float32)


def pack_spectral(w1, b1, w2, b2, one):
    import numpy as np
    t = np.zeros((BLOCKS, ROWS, W_COLS), np.float32)
    for row in range(2):
        rows = slice(row * BLOCK, (row + 1) * BLOCK)
        for to in range(2):
            t[:, rows, to * BLOCK:(to + 1) * BLOCK] = w1[row ^ to]
            t[:, rows, SECOND + to * BLOCK:SECOND + (to + 1) * BLOCK] = w2[row ^ to]
        t[:, ONE_ROW, SECOND + row * BLOCK:SECOND + (row + 1) * BLOCK] = b2[row]
        t[:, rows, BIAS] = b1[row]
    t[:, ONE_ROW, BIAS] = one
    return t


def kernel(**inputs):
    import numpy as np
    import concourse.bacc as bacc
    from concourse.bass_utils import run_bass_kernel_spmd

    a = {k: np.asarray(t) for k, t in inputs.items()}

    def all_blocks(t):
        return np.broadcast_to(t, (BLOCKS,) + t.shape)

    spectral = np.stack([
        pack_spectral(a["L0_conv_w1"], a["L0_conv_b1"], a["L0_conv_w2"], a["L0_conv_b2"], 1.0),
        pack_spectral(a["L1_conv_w1"], a["L1_conv_b1"], a["L1_conv_w2"], a["L1_conv_b2"], ONE_GELU),
        pack_spectral([all_blocks(a["L2_conv_w1r"].T), all_blocks(a["L2_conv_w1i"].T)],
                      [all_blocks(a["L2_conv_b1"][:, n]) for n in range(2)],
                      [all_blocks(a["L2_conv_w2r"].T), all_blocks(a["L2_conv_w2i"].T)],
                      [all_blocks(a["L2_conv_b2"][:, n]) for n in range(2)], 1.0),
        pack_spectral([a["L3_conv_w1"][..., n] for n in range(2)], [a["L3_conv_b1"][..., n] for n in range(2)],
                      [a["L3_conv_w2"][..., n] for n in range(2)], [a["L3_conv_b2"][..., n] for n in range(2)], 1.0)])
    arrays = {
        "x": a["x"].reshape(BATCH, SIDE * SIDE, CHANNELS),
        "consts": host_constants(),
        "spectral": spectral,
        "ln1": np.stack([a["L1_conv_ln1_g"], a["L1_conv_ln1_b"]]),
        "lncol": np.stack([a["L1_conv_ln1_g"], a["L1_conv_ln1_b"]], 1).reshape(PAIRS, PAIR, 2).transpose(1, 0, 2),
        "cols": np.concatenate([a["L1_conv_mlp_b1"].reshape(HC, P), a["L1_conv_ln2_g"].reshape(KC, P),
                                a["L1_conv_ln2_b"].reshape(KC, P)]).T,
        "w1": a["L1_conv_mlp_w1"],
        "w2": a["L1_conv_mlp_w2"],
        "b2": a["L1_conv_mlp_b2"],
    }
    arrays = {f"in_{k}": np.ascontiguousarray(t) for k, t in arrays.items()}
    nc = bacc.Bacc("TRN2", target_bir_lowering=False, num_devices=1)
    args = [nc.dram_tensor(k, t.shape, mybir.dt.from_np(t.dtype), kind="ExternalInput").ap() for k, t in arrays.items()]
    out = nc.dram_tensor("out", (BATCH, SIDE * SIDE, CHANNELS), F32, kind="ExternalOutput").ap()
    build(nc, *args, out)
    r = run_bass_kernel_spmd(nc, [arrays], core_ids=[0])
    return np.asarray(r.results[0]["out"]).reshape(BATCH, SIDE, SIDE, CHANNELS)
```

```python
from contextlib import ExitStack

import concourse.bass as bass
from concourse import mybir

ALU = mybir.AluOpType
ACT = mybir.ActivationFunctionType
F32 = mybir.dt.float32
F32R = mybir.dt.float32r

P = 128
BATCH, SIDE, CHANNELS = 2, 64, 384
BLOCKS, BLOCK = 8, 48
PAIR = 2 * BLOCK
PAIRS = CHANNELS // PAIR
ROWPAIRS = SIDE * SIDE // P
CHUNK = 4
CHUNKS = ROWPAIRS // CHUNK
HALF = SIDE // 2
HIDDEN = 4 * CHANNELS
KC, HC = CHANNELS // P, HIDDEN // P
TOKENS = 4 * P
TILES = BATCH * SIDE * SIDE // TOKENS
LAG = 2
WPART = 2 * CHANNELS
WPARTS = KC * HIDDEN // WPART
LAMBDA = 0.01
ONE_ROW = PAIR
ONE_GELU = 8.0
LN_EPS = 1e-5

(C_D1, C_ID, C_D2, C_D2A, C_D2B, C_D5, C_D6) = [P * n for n in range(7)]
C_D5P, C_D5P0, C_SIGN = 7 * P, 9 * P, 11 * P
C_COLS = C_SIGN + 5
ROWS = PAIR + 1
SECOND, BIAS = ROWS, ROWS + PAIR
W_COLS = BIAS + 1
PARTS = 4
PART_CHUNKS = CHUNKS // PARTS
W_STEPS = 8
STAGES = 6
POST_SKEW = 2
POST_STEPS = CHUNKS + POST_SKEW
POST_BESIDE = (((), (2,)), ((3,), (4, 5)), ((6,), (7,)), ((8, 9), ()))
F1_BESIDE = ((0,), (1,), (2, 3), (4, 5, 6), (7,))


class Layer:

    def __init__(self, index, kh, forward, inverse, act, shrink, norm, chain_base):
        self.index, self.kh = index, kh
        self.forward, self.inverse = forward, inverse
        self.act, self.shrink, self.norm = act, shrink, norm
        if kh == SIDE:
            self.groups = [(0, 1, 1, [(0, SIDE, C_D2A, [0]), (SIDE, SIDE, C_D2B, [0])],
                            [(0, 0, C_D5, SIDE, 0, True, True), (1, 0, C_D5, SIDE, SIDE, True, True)])]
            for s in range(1, HALF, 4):
                n = min(4, HALF - s)
                self.groups.append((s, n, 2, [(0, SIDE, C_D2, [0, 2]), (SIDE, SIDE, C_D2, [1, min(3, n - 1)])],
                                    [(j % 2, j // 2, C_D5, P, j * P, True, True) for j in range(n)]))
        else:
            self.groups = []
            for s in range(0, HALF, 4):
                rows = [(j * HALF, HALF, C_D2A if s + j == 0 else C_D2, [j]) for j in range(4)]
                items = [(j, 0, C_D5P0 if s + j == 0 else C_D5P, 2 * P, 2 * j * P, True, True) for j in range(2)]
                self.groups.append((s, 4, 1, rows, items))
        self.units = index * 2 * PAIRS
        self.chain = chain_base
        self.n = len(self.groups)
        self.split = kh == SIDE
        self.skip = 0


def iterate(engine, count, body):
    body(0, False)
    with engine.Fori(1, count - 1) as i:
        body(i, False)
    body(count - 1, True)


def first_of(i):
    return isinstance(i, int) and i == 0


def wait_past(engine, semaphore, value):
    if not isinstance(value, int) or value > 0:
        engine.wait_ge(semaphore, value)


def make_layers():
    layers, base = [], 0
    for index, (kh, fwd, inv, act, shrink, norm) in enumerate([
            (SIDE, 1.0, 1.0 / (SIDE * SIDE), ACT.Relu, True, False),
            (HALF, 1.0 / SIDE, 1.0 / SIDE, ACT.Gelu, False, True),
            (SIDE, 1.0 / SIDE, 1.0 / SIDE, ACT.Relu, True, False),
            (SIDE, 1.0 / SIDE, 1.0 / SIDE, ACT.Relu, True, False)]):
        layers.append(Layer(index, kh, fwd, inv, act, shrink, norm, base))
        base += 2 * PAIRS * layers[-1].n
        if index > 1:
            layers[-1].skip = 2 * PAIRS * layers[1].n
    return layers


def build(nc, x, consts, spectral, ln1, lncol_in, cols, w1, w2, b2, out):
    layers = make_layers()
    with ExitStack() as ctx:
        def sb(name, shape):
            return ctx.enter_context(nc.sbuf_tensor(name, shape, F32))

        def sbr(name, shape):
            return ctx.enter_context(nc.sbuf_tensor(name, shape, F32R))

        def sem(name):
            return ctx.enter_context(nc.semaphore(name))

        after = [nc.dram_tensor(f"after_{n}", (BATCH, SIDE * SIDE, CHANNELS), F32).ap() for n in range(4)]
        layer_in = [x, after[0], after[2], after[3]]
        layer_out = [after[0], after[1], after[3], out]

        UNIT = ROWPAIRS * PAIR
        const = sb("const", [P, C_COLS])
        lnrow = sb("lnrow", [P, 2, CHANNELS])
        lncol = sb("lncol", [P, PAIRS, 2])
        gcol = sb("gcol", [P, 2])
        colp = sb("colp", [P, HC + 2 * KC])
        stat = sb("stat", [P, 4, 6])
        mv = sb("mv", [P, BATCH * ROWPAIRS, 2])
        rstd = sb("rstd", [P, BATCH * ROWPAIRS])
        mv2 = sb("mv2", [P, 2, 4, 2])
        rstd2 = sb("rstd2", [P, 2, 4])
        power = sb("power", [P, 1])
        eps = sb("eps", [P, 1])
        counts = sb("counts", [P, 4])
        d6h, d6l = sbr("d6h", [P, P]), sbr("d6l", [P, P])
        w1h, w1l = sbr("w1h", [P, KC * HIDDEN]), sbr("w1l", [P, KC * HIDDEN])
        w2h, w2l = sbr("w2h", [P, KC * HIDDEN]), sbr("w2l", [P, KC * HIDDEN])

        with ExitStack() as scope:
            def sb(name, shape, dtype=F32):
                return scope.enter_context(nc.sbuf_tensor(name, shape, dtype))

            with nc.sbuf_tensor("wraw", [P, WPART], F32) as wraw, \
                    nc.sbuf_tensor("st", [P, BATCH * ROWPAIRS, PAIRS, 6], F32) as st:
                pass
            sb("early", [P, 2 * 4 * CHANNELS])
            xs1 = sb("xs1", [P, UNIT])
            res = sb("res", [P, 2, UNIT])
            y = sb("y", [P, HALF, 2, SIDE])
            z = sb("z", [P, 2, 4 * PAIR])
            zs = sb("zs", [P, 2, 4 * PAIR])
            with nc.sbuf_tensor("zf", [P, 2, 2, 2 * P], F32) as zf:
                pass
            zfh, zfl = sb("zfh", [P, 2, 2, 2 * P], F32R), sb("zfl", [P, 2, 2, 2 * P], F32R)
            h = sb("h", [P, 2, 2, 2 * P])
            clamp = sb("clamp", [P, 4 * PAIR])
            u = sb("u", [P, 2, 2, 2 * PAIR])
            v = sb("v", [P, SIDE, 2, HALF])
            vth, vtl = sb("vth", [P, 2, CHUNK * PAIR], F32R), sb("vtl", [P, 2, CHUNK * PAIR], F32R)
            wstage = sb("wstage", [P, 2, W_COLS])
            w = sb("w", [P, 2, W_COLS])
            wh, wl = sb("wh", [P, 2, ROWS], F32R), sb("wl", [P, 2, ROWS], F32R)
            xs = (sb("xs0", [P, UNIT]), xs1)
        with ExitStack() as scope:
            def sb(name, shape, dtype=F32):
                return scope.enter_context(nc.sbuf_tensor(name, shape, dtype))

            xm = sb("xm", [P, 2, 4, CHANNELS])
            g = sb("g", [P, 2, TOKENS])
            gl = sb("gl", [P, 4, TOKENS], F32R)
            xh = sb("xh", [P, 2, 4, CHANNELS])
            om = sb("om", [P, 2, 4, CHANNELS])
            mt = sb("mt", [P, KC, TOKENS])
            mth, mtl = sb("mth", [P, 2, KC, TOKENS], F32R), sb("mtl", [P, 2, KC, TOKENS], F32R)
            gh = sb("gh", [P, 4, TOKENS], F32R)
            b2row = sb("b2row", [P, CHANNELS])

        ps = ctx.enter_context(nc.psum_tensor("ps", [P, 8, 512], F32))
        T_BANK, F2_BANK, T2_BANK, M1_BANK, M2_BANK, F5_BANK = range(6)
        F1_BANKS = (6, 7)
        TT_BANKS = (6, M1_BANK, 7, 6, M1_BANK, 7, 6, 7)
        F6_BANKS = (M2_BANK, F5_BANK)
        TURN_BANKS, MM1_BANKS, MM2_BANKS = (6, 7), (4, 5), (0, 1, 2, 3)

        s_first, s_const, s_wts = sem("s_first"), sem("s_const"), sem("s_wts")
        basis_high, basis_low = sem("basis_high"), sem("basis_low")
        x_loaded = [[sem(f"x_loaded{b}{part}") for part in range(PARTS)] for b in range(BATCH)]
        stored = [[sem(f"stored{b}{part}") for part in range(PARTS)] for b in range(BATCH)]
        w_loaded, w_ready = sem("w_loaded"), sem("w_ready")
        f1_done, t_done, f2_done, m1_done = sem("f1_done"), sem("t_done"), sem("f2_done"), sem("m1_done")
        m2_done, f5_done, tt_done, f6_done = sem("m2_done"), sem("f5_done"), sem("tt_done"), sem("f6_done")
        y_ready, z_ready, zf_ready, h_ready = sem("y_ready"), sem("z_ready"), sem("zf_ready"), sem("h_ready")
        zf_low = sem("zf_low")
        clamped, u_ready, v_ready = sem("clamped"), sem("u_ready"), sem("v_ready")
        vt_high, vt_low, res_ready = sem("vt_high"), sem("vt_low"), sem("res_ready")
        t2_done, zs_ready = sem("t2_done"), sem("zs_ready")
        gcol_ready, shifted = sem("gcol_ready"), sem("shifted")
        centred, gained, ln_step, sum_ready = sem("centred"), sem("gained"), sem("ln_step"), sem("sum_ready")
        st_done, mv_ready, rs_step, rstd_ready = sem("st_done"), sem("mv_ready"), sem("rs_step"), sem("rstd_ready")
        wpart_loaded, wpart_high, wpart_low = sem("wpart_loaded"), sem("wpart_high"), sem("wpart_low")
        m_loaded = [sem("m_loaded0"), sem("m_loaded1")]
        m_stored = [sem("m_stored0"), sem("m_stored1")]
        st2_done, mv2_ready, rs2_step, rstd2_ready = sem("st2_done"), sem("mv2_ready"), sem("rs2_step"), sem("rstd2_ready")
        xh_ready, skip_ready = sem("xh_ready"), sem("skip_ready")
        turned, mt_ready, mt_high, mt_low = sem("turned"), sem("mt_ready"), sem("mt_high"), sem("mt_low")
        mm1_done, g_ready, g_high, g_low = sem("mm1_done"), sem("g_ready"), sem("g_high"), sem("g_low")
        mm2_done, om_ready = sem("mm2_done"), sem("om_ready")

        def basis(col, width=P):
            return const[:, col:col + width]

        def wpart(first, second, n):
            m = n % WPARTS
            return (first if n < WPARTS else second)[:, m * WPART:(m + 1) * WPART]

        ident = basis(C_ID)
        SPLIT_STEPS = {7 + n: n for n in range(WPARTS)}
        AGGREGATE_AT = (6, 4)
        TURN_AT = 8

        def unit_view(a, b, i):
            return a[b].rearrange("(r p) c -> p r c", p=P)[:, :, bass.ds(i * PAIR, PAIR)]

        def part_view(a, b, i, part):
            n = ROWPAIRS // PARTS
            return unit_view(a, b, i)[:, part * n:(part + 1) * n]

        def part_buffer(t, part):
            n = UNIT // PARTS
            return t[:, part * n:(part + 1) * n].rearrange("p (r c) -> p r c", c=PAIR)

        def tile_view(a, n):
            return a.rearrange("b (n j p) c -> p (b n) j c", p=P, j=4)[:, bass.ds(n, 1)].rearrange("p o j c -> p (o j) c")

        block = ctx.enter_context(nc.Block())

        @block.sync
        def _(sp):
            sp.dma_start(const[:, 0:C_D2], consts[:, 0:C_D2]).then_inc(s_first, 16)

            def load_weights(L, i):
                sp.dma_start(wstage[0:ROWS, :, :],
                             spectral[L.index].rearrange("(g k) p n -> p g k n", k=2)[:, bass.ds(i, 1)]
                             .rearrange("p o k n -> p (o k) n")).then_inc(w_loaded, 16)

            def load_part(L, b, i, part):
                sp.dma_start(part_buffer(xs[b], part),
                             part_view(layer_in[L.index], b, i, part)).then_inc(x_loaded[b][part], 16)

            def spectral_layer(L, loaded, following):
                if not loaded:
                    for part in range(PARTS):
                        load_part(L, 0, 0, part)
                    sp.dma_start(const[:, C_D2:], consts[:, C_D2:]).then_inc(s_const, 16)
                    load_weights(L, 0)
                    for part in range(PARTS):
                        load_part(L, 1, 0, part)
                if L.index == 0:
                    split_loads(0)

                def body(i, last):
                    if not last or following:
                        sp.wait_ge(w_ready, W_STEPS * (PAIRS * L.index + 1) + i * W_STEPS)
                        load_weights(following if last else L, 0 if last else i + 1)
                    for b in range(BATCH):
                        if L.index == 1 and last and b == 1:
                            for part in range(PARTS):
                                sp.wait_ge(stored[0][part], 16 * PAIRS * (L.index + 1))
                            for r in range(2):
                                sp.dma_start(xm[:, r], tile_view(after[1], r)).then_inc(m_loaded[r], 16)
                        for part in range(PARTS):
                            sp.wait_ge(res_ready, CHUNKS * (L.units + b) + PART_CHUNKS * (part + 1) + i * (2 * CHUNKS))
                            sp.dma_start(part_view(layer_out[L.index], b, i, part),
                                         part_buffer(res[:, b], part)).then_inc(stored[b][part], 16)
                            if not last:
                                load_part(L, b, i + 1, part)
                            elif following:
                                sp.wait_ge(stored[b][part], 16 * (PAIRS * L.index + 1))
                                load_part(following, b, 0, part)
                        if L.index == 0 and first_of(i) and b == 0:
                            split_loads(1)

                iterate(sp, PAIRS, body)

            def split_loads(matrix):
                for m in range(WPARTS):
                    if matrix or m:
                        sp.wait_ge(wpart_low, matrix * WPARTS + m)
                    if matrix == 0:
                        src = w1[m // 2 * P:(m // 2 + 1) * P, m % 2 * WPART:(m % 2 + 1) * WPART]
                    else:
                        src = w2[2 * m * P:2 * (m + 1) * P, :].rearrange("(k p) n -> p k n", p=P)
                    dst = wraw[:, :] if matrix == 0 else wraw[:, :].rearrange("p (k n) -> p k n", k=2)
                    sp.dma_start(dst, src).then_inc(wpart_loaded, 16)
                if matrix:
                    sp.dma_start(lnrow[:, :, :], ln1.rearrange("a c -> (a c)").partition_broadcast(P)
                                 .rearrange("p (a c) -> p a c", a=2)).then_inc(s_wts, 16)
                    sp.dma_start(lncol[0:PAIR, :, :], lncol_in).then_inc(s_wts, 16)
                    sp.dma_start(colp[:, :], cols).then_inc(s_wts, 16)

            def token_mlp_moves():
                for part in range(PARTS):
                    sp.wait_ge(stored[1][part], 16 * PAIRS * 2)

                sp.dma_start(b2row[:, :], b2.partition_broadcast(P)).then_inc(s_wts, 16)

                def body(i, last):
                    for r in range(2):
                        if last and r == 1:
                            for n in range(2):
                                sp.wait_ge(m_stored[n], 16 * TILES // (2 * BATCH))
                            for part in range(PARTS):
                                load_part(layers[2], 0, 0, part)
                            load_weights(layers[2], 0)
                        sp.wait_ge(om_ready, 4 * (r + 1) + i * 8)
                        sp.dma_start(tile_view(after[2], 2 * i + r), om[:, r]).then_inc(m_stored[r], 16)
                        if not last:
                            sp.dma_start(xm[:, r], tile_view(after[1], 2 * i + (2 + r))).then_inc(m_loaded[r], 16)

                iterate(sp, TILES // 2, body)
                for r in range(2):
                    sp.wait_ge(m_stored[r], 16 * TILES // 2)
                for part in range(PARTS):
                    load_part(layers[2], 1, 0, part)

            spectral_layer(layers[0], False, layers[1])
            spectral_layer(layers[1], True, None)
            token_mlp_moves()
            spectral_layer(layers[2], True, layers[3])
            spectral_layer(layers[3], True, None)
            for b in range(BATCH):
                for part in range(PARTS):
                    sp.wait_ge(stored[b][part], 16 * PAIRS * 4)

        @block.tensor
        def _(pe):
            pe.wait_ge(s_first, 16)
            def f1(L, b, i, k):
                if L.norm:
                    pe.wait_ge(centred, CHUNKS * b + k + 1 + i * (2 * CHUNKS))
                    src = res[:, b]
                else:
                    if k % PART_CHUNKS == 0:
                        pe.wait_ge(x_loaded[b][k // PART_CHUNKS], 16 * (PAIRS * L.index + 1) + i * 16)
                    src = xs[b]
                if k >= 2:
                    pe.wait_ge(y_ready, CHUNKS * (L.units + b) + k - 1 + i * (2 * CHUNKS))
                for j in range(CHUNK):
                    r = CHUNK * k + j
                    mm = pe.matmul(ps[0:PAIR, F1_BANKS[k % 2], j * P:(j + 1) * P],
                                   src[:, r * PAIR:(r + 1) * PAIR], basis(C_D1), start=True, stop=True)
                mm.then_inc(f1_done, 1)

            def post(L, b, i, t, beside):
                base = CHUNKS * (L.units + b)
                if t == 0:
                    pe.wait_ge(v_ready, L.chain + (b + 1) * L.n + i * (2 * L.n))
                    if beside:
                        pe.wait_ge(y_ready, base + 2 * CHUNKS - 1 + i * (2 * CHUNKS))
                    elif L.norm:
                        pe.wait_ge(mt_ready, KC)

                def to_frequencies():
                    if t < CHUNKS:
                        for j in range(CHUNK):
                            r = 2 * (CHUNK * t + j)
                            mm = pe.transpose(ps[:, TT_BANKS[t], j * PAIR:(j + 1) * PAIR],
                                              v[0:PAIR, r:r + 2].rearrange("p a b c -> p (a b c)"),
                                              ident[0:PAIR, 0:PAIR])
                        mm.then_inc(tt_done, 1)

                def to_columns():
                    k = t - POST_SKEW
                    if k >= 0:
                        pe.wait_ge(vt_low, base + k + 1 + i * (2 * CHUNKS))
                        if k >= 2:
                            pe.wait_ge(res_ready, base + k - 1 + i * (2 * CHUNKS))
                        for m, (d, data) in enumerate([(d6h, vth), (d6h, vtl), (d6l, vth)]):
                            mm = pe.matmul(ps[:, F6_BANKS[k % 2], 0:CHUNK * PAIR], d[:, :], data[:, k % 2, :],
                                           start=m == 0, stop=m == 2)
                        mm.then_inc(f6_done, 1)

                for part in (to_frequencies, to_columns) if t == POST_SKEW else (to_columns, to_frequencies):
                    part()

            def turn(r, i, k):
                if k == 0:
                    pe.wait_ge(xh_ready, 4 * (r + 1) + i * 8)
                if k >= 2:
                    pe.wait_ge(mt_ready, KC * r + k - 1 + i * (2 * KC))
                for j in range(4):
                    mm = pe.transpose(ps[:, TURN_BANKS[k % 2], j * P:(j + 1) * P],
                                      xh[:, r, j, k * P:(k + 1) * P], ident)
                mm.then_inc(turned, 1)

            def chain(L, b, i, before, after):
                done = L.chain + b * L.n
                step = 2 * L.n
                if before:
                    before_done = CHUNKS * (before[0].units + before[1] + 1)
                    for p in range(POST_SKEW):
                        post(*before, p, True)
                for t in range(L.n + STAGES - 1):
                    k = t - 5
                    if 0 <= k < L.n:
                        pe.wait_ge(u_ready, done + k + 1 + i * step)
                        if k == 0 and before:
                            pe.wait_ge(res_ready, before_done + before[2] * (2 * CHUNKS))
                        if k >= 1:
                            pe.wait_ge(v_ready, done + k + i * step)
                        for half, pos, col, width, to, first, final in L.groups[k][4]:
                            mm = pe.matmul(ps[0:PAIR, F5_BANK, to:to + width],
                                           u[:, k % 2, half, pos * PAIR:(pos + 1) * PAIR],
                                           basis(col, width), start=first, stop=final)
                        mm.then_inc(f5_done, 1)
                    k = t - 4
                    if 0 <= k < L.n:
                        pe.wait_ge(h_ready, 2 * (done + k + 1) + i * (2 * step))
                        if k == 0 and before:
                            pe.wait_ge(res_ready, before_done - 1 + before[2] * (2 * CHUNKS))
                        npos = L.groups[k][2]
                        to = ps[:, M2_BANK, 0:npos * 2 * PAIR].rearrange("p (a q n c) -> p a q n c", a=2, q=npos, n=2)
                        for pos in range(npos):
                            for n in range(2):
                                mm = pe.matmul(to[:, :, pos, n], h[0:ROWS, k % 2, n, pos * P:(pos + 1) * P],
                                               w[0:ROWS, n, SECOND:BIAS].rearrange("p (a c) -> p a c", a=2),
                                               start=True, stop=True)
                        mm.then_inc(m2_done, 1)
                    k = t - 3
                    if 0 <= k < L.n:
                        if L.split:
                            pe.wait_ge(zf_low, done - L.skip + k + 1 + i * step)
                        else:
                            pe.wait_ge(zf_ready, done + k + 1 + i * step)
                        if k == 0 and b == 0:
                            pe.wait_ge(w_ready, W_STEPS * (PAIRS * L.index + 1) + i * W_STEPS)
                        width = L.groups[k][2] * P
                        for n in range(2):
                            to = ps[0:ROWS, M1_BANK, n * 2 * P:n * 2 * P + width]
                            parts = [(wh, zfh), (wh, zfl), (wl, zfh)] if L.split else [(w, zf)]
                            for m, (weight, data) in enumerate(parts):
                                mm = pe.matmul(to, weight[0:PAIR, n, 0:ROWS], data[0:PAIR, k % 2, n, 0:width],
                                               start=m == 0, stop=m == len(parts) - 1)
                        mm.then_inc(m1_done, 1)
                    k = t - 2
                    if 0 <= k < L.n:
                        pe.wait_ge(zs_ready, done + k + 1 + i * step)
                        for pos in range(L.groups[k][2]):
                            for n in range(2):
                                at, to = (2 * pos + n) * PAIR, (2 * n + pos) * P
                                mm = pe.transpose(ps[0:PAIR, T2_BANK, to:to + P], zs[:, k % 2, at:at + PAIR], ident)
                        mm.then_inc(t2_done, 1)
                    k = t - 1
                    if 0 <= k < L.n:
                        pe.wait_ge(z_ready, done + k + 1 + i * step)
                        npos = L.groups[k][2]
                        to = ps[:, F2_BANK, 0:npos * 2 * PAIR].rearrange("p (q n a c) -> p q n a c", q=npos, n=2, a=2)
                        src = z[:, k % 2, :].rearrange("p (s n c) -> p s n c", n=2, c=BLOCK)
                        for ri in range(2):
                            for p0, rows, col, slots in L.groups[k][3]:
                                stop = slots[-1] + 1
                                by = slots[1] - slots[0] if len(slots) > 1 else 1
                                mm = pe.matmul(to[p0:p0 + rows, :, :, ri], basis(col + ri * SIDE, rows),
                                               src[:, slots[0]:stop:by], start=True, stop=True)
                        mm.then_inc(f2_done, 1)
                    if before and t < len(POST_BESIDE):
                        for p in POST_BESIDE[t][0]:
                            post(*before, p, True)
                    k = t
                    if k < L.n:
                        if k == 0:
                            if L.norm:
                                pe.wait_ge(shifted, b + 1 + i * 2)
                            else:
                                pe.wait_ge(y_ready, CHUNKS * (L.units + b + 1) + i * (2 * CHUNKS))
                        s0, slots = L.groups[k][0:2]
                        for j in range(slots):
                            mm = pe.transpose(ps[:, T_BANK, j * PAIR:(j + 1) * PAIR],
                                              y[0:PAIR, s0 + j].rearrange("p a b -> p (a b)"),
                                              ident[0:PAIR, 0:PAIR])
                        mm.then_inc(t_done, 1)
                    if before and t < len(POST_BESIDE):
                        for p in POST_BESIDE[t][1]:
                            post(*before, p, True)
                    if after and t >= L.n:
                        for p in F1_BESIDE[t - L.n]:
                            f1(*after, p)
                    if L.norm and not after and 0 <= t - L.n - 2 < KC:
                        turn(0, 0, t - L.n - 2)

            def spectral_layer(L, previous, following):
                if not previous:
                    for k in range(CHUNKS):
                        f1(L, 0, 0, k)
                    if L.index > 0:
                        pe.wait_ge(om_ready, 4 * TILES)
                    else:
                        pe.wait_ge(s_const, 16)
                        pe.wait_ge(basis_low, 1)

                def body(i, last):
                    before = (previous, 1, PAIRS - 1) if first_of(i) else (L, 1, i - 1)
                    after = (L, 0, i + 1) if not last else (following, 0, 0)
                    chain(L, 0, i, before if before[0] else None, (L, 1, i))
                    chain(L, 1, i, (L, 0, i), after if after[0] else None)

                iterate(pe, PAIRS, body)
                if not following:
                    for t in range(POST_STEPS):
                        post(L, 1, PAIRS - 1, t, False)

            def token_mlp():
                def first(r, i, n):
                    if n == 0:
                        pe.wait_ge(mt_low, KC * (r + 1) + i * (2 * KC))
                    if n >= 2:
                        pe.wait_ge(g_ready, HC * r + n - 1 + i * (2 * HC))
                    for k in range(KC):
                        at = slice(k * HIDDEN + n * P, k * HIDDEN + (n + 1) * P)
                        for m, (a, b) in enumerate([(w1h, mth), (w1h, mtl), (w1l, mth)]):
                            mm = pe.matmul(ps[:, MM1_BANKS[n % 2], :], a[:, at], b[:, r, k, :],
                                           start=k == 0 and m == 0, stop=k == KC - 1 and m == 2)
                    mm.then_inc(mm1_done, 1)

                def second(r, i, n):
                    pe.wait_ge(g_low, HC * r + n + 1 + i * (2 * HC))
                    if n == 0:
                        wait_past(pe, om_ready, 4 * r + i * 8)
                    at = slice(n * CHANNELS, (n + 1) * CHANNELS)
                    for j in range(4):
                        part = slice(j * P, (j + 1) * P)
                        for m, (a, b) in enumerate([(gh, w2h), (gh, w2l), (gl, w2h)]):
                            mm = pe.matmul(ps[:, MM2_BANKS[j], 0:CHANNELS], a[:, n % 4, part], b[:, at],
                                           start=n == 0 and m == 0, stop=n == HC - 1 and m == 2)
                        if n == HC - 1:
                            mm.then_inc(mm2_done, 1)

                def tile(r, i, following):
                    for t in range(HC + LAG):
                        if t < HC:
                            first(r, i, t)
                        if 0 <= t - TURN_AT < KC and following:
                            turn(*following, t - TURN_AT)
                        if t >= LAG:
                            second(r, i, t - LAG)

                def body(i, last):
                    tile(0, i, (1, i))
                    tile(1, i, None if last else (0, i + 1))

                pe.wait_ge(res_ready, CHUNKS * layers[2].units)
                iterate(pe, TILES // 2, body)

            spectral_layer(layers[0], None, layers[1])
            spectral_layer(layers[1], layers[0], None)
            token_mlp()
            spectral_layer(layers[2], None, layers[3])
            spectral_layer(layers[3], layers[2], None)

        @block.scalar
        def _(act):
            def f1(L, b, i, k):
                act.wait_ge(f1_done, CHUNKS * (L.units + b) + k + 1 + i * (2 * CHUNKS))
                r = 2 * CHUNK * k
                to = y[0:PAIR].rearrange("p k a r -> p r a k")[:, r:r + 2 * CHUNK]
                src = ps[0:PAIR, F1_BANKS[k % 2], :].rearrange("p (r a k) -> p r a k", a=2, k=HALF)
                if not L.norm:
                    act.activation(to, src, ACT.Copy).then_inc(y_ready, 1)
                    return
                if k == 0 and b == 0:
                    act.wait_ge(gcol_ready, 1 + i)
                act.activation(to, src, ACT.Identity, scale=gcol[0:PAIR, 0:1]).then_inc(y_ready, 1)
                if k == CHUNKS - 1:
                    act.wait_ge(y_ready, CHUNKS * (L.units + b + 1) + i * (2 * CHUNKS))
                    act.activation(y[0:PAIR, 0, 0, :], y[0:PAIR, 0, 0, :], ACT.Identity,
                                   bias=gcol[0:PAIR, 1:2]).then_inc(shifted, 1)

            def post(L, b, i, t):
                if t < CHUNKS:
                    act.wait_ge(tt_done, CHUNKS * (L.units + b) + t + 1 + i * (2 * CHUNKS))
                    if t >= 2:
                        act.wait_ge(f6_done, CHUNKS * (L.units + b) + t - 1 + i * (2 * CHUNKS))
                    act.activation(vth[:, t % 2, :], ps[:, TT_BANKS[t], 0:CHUNK * PAIR],
                                   ACT.Copy).then_inc(vt_high, 1)

            def turn(r, i, k):
                act.wait_ge(turned, KC * r + k + 1 + i * (2 * KC))
                act.activation(mt[:, k, :], ps[:, TURN_BANKS[k % 2], :], ACT.Identity,
                               scale=colp[:, HC + k:HC + k + 1],
                               bias=colp[:, HC + KC + k:HC + KC + k + 1]).then_inc(mt_ready, 1)

            def chain(L, b, i, before, after):
                done = L.chain + b * L.n
                step = 2 * L.n
                if before:
                    for p in range(POST_SKEW):
                        post(*before, p)
                for t in range(L.n + STAGES - 1):
                    k = t - 5
                    if 0 <= k < L.n:
                        act.wait_ge(f5_done, done + k + 1 + i * step)
                        s0, slots = L.groups[k][0:2]
                        act.activation(v[0:PAIR].rearrange("p r a k -> p k a r")[:, s0:s0 + slots],
                                       ps[0:PAIR, F5_BANK, 0:slots * P].rearrange("p (k a r) -> p k a r", a=2, r=SIDE),
                                       ACT.Copy, scale=L.inverse).then_inc(v_ready, 1)
                    k = t - 3
                    if 0 <= k < L.n:
                        act.wait_ge(m1_done, done + k + 1 + i * step)
                        width = L.groups[k][2] * P
                        for n in range(2):
                            act.activation(h[0:ROWS, k % 2, n, 0:width],
                                           ps[0:ROWS, M1_BANK, n * 2 * P:n * 2 * P + width],
                                           L.act, bias=w[0:ROWS, n, BIAS:W_COLS]).then_inc(h_ready, 1)
                    k = t - 2
                    if 0 <= k < L.n:
                        act.wait_ge(t2_done, done + k + 1 + i * step)
                        width = L.groups[k][2] * P
                        act.activation((zfh if L.split else zf)[0:PAIR, k % 2, :, 0:width],
                                       ps[0:PAIR, T2_BANK, :].rearrange("p (n m) -> p n m", n=2)[:, :, 0:width],
                                       ACT.Copy).then_inc(zf_ready, 1)
                    if before and t < len(POST_BESIDE):
                        for p in POST_BESIDE[t][0]:
                            post(*before, p)
                    k = t
                    if k < L.n:
                        act.wait_ge(t_done, done + k + 1 + i * step)
                        n = L.groups[k][1] * PAIR
                        act.activation(z[:, k % 2, 0:n], ps[:, T_BANK, 0:n], ACT.Copy).then_inc(z_ready, 1)
                    if before and t < len(POST_BESIDE):
                        for p in POST_BESIDE[t][1]:
                            post(*before, p)
                    if after and t >= L.n:
                        for p in F1_BESIDE[t - L.n]:
                            f1(*after, p)
                    if L.norm and not after and 0 <= t - L.n - 2 < KC:
                        if t == L.n + 2:
                            act.wait_ge(s_wts, 48)
                        turn(0, 0, t - L.n - 2)
                    if L.index == 0 and first_of(i) and t in SPLIT_STEPS:
                        n = b * WPARTS + SPLIT_STEPS[t]
                        act.wait_ge(wpart_loaded, 16 * (n + 1))
                        act.activation(wpart(w1h, w2h, n), wraw[:, :], ACT.Copy).then_inc(wpart_high, 1)

            def spectral_layer(L, previous, following):
                if not previous:
                    for k in range(CHUNKS):
                        f1(L, 0, 0, k)

                def body(i, last):
                    before = (previous, 1, PAIRS - 1) if first_of(i) else (L, 1, i - 1)
                    after = (L, 0, i + 1) if not last else (following, 0, 0)
                    chain(L, 0, i, before if before[0] else None, (L, 1, i))
                    chain(L, 1, i, (L, 0, i), after if after[0] else None)

                iterate(act, PAIRS, body)
                if not following:
                    for t in range(POST_STEPS):
                        post(L, 1, PAIRS - 1, t)

            def token_mlp():
                def first(r, i, n):
                    act.wait_ge(mm1_done, HC * r + n + 1 + i * (2 * HC))
                    wait_past(act, g_low, HC * r + n - 1 + i * (2 * HC))
                    act.activation(g[:, n % 2, :], ps[:, MM1_BANKS[n % 2], :], ACT.Gelu,
                                   bias=colp[:, n:n + 1]).then_inc(g_ready, 1)
                    act.wait_ge(g_ready, HC * r + n + 1 + i * (2 * HC))
                    act.activation(gh[:, n % 4, :], g[:, n % 2, :], ACT.Copy).then_inc(g_high, 1)

                def tile(r, i, following):
                    for t in range(HC):
                        first(r, i, t)
                        if 0 <= t - TURN_AT < KC and following:
                            turn(*following, t - TURN_AT)

                def body(i, last):
                    tile(0, i, (1, i))
                    tile(1, i, None if last else (0, i + 1))

                act.wait_ge(res_ready, CHUNKS * layers[2].units)
                iterate(act, TILES // 2, body)

            spectral_layer(layers[0], None, layers[1])
            spectral_layer(layers[1], layers[0], None)
            token_mlp()
            spectral_layer(layers[2], None, layers[3])
            spectral_layer(layers[3], layers[2], None)

        @block.vector
        def _(dve):
            dve.wait_ge(s_const, 16)
            dve.tensor_copy(d6h[:, :], basis(C_D6)).then_inc(basis_high, 1)
            dve.wait_ge(basis_high, 1)
            dve.tensor_tensor(d6l[:, :], basis(C_D6), d6h[:, :], ALU.subtract).then_inc(basis_low, 1)

            def chain(L, b, i, before, last):
                done = L.chain + b * L.n
                step = 2 * L.n
                urgent = L.norm or last
                shrunk = done - L.skip
                if before:
                    for p in range(POST_SKEW):
                        post(*before, p)
                for t in range(L.n + STAGES - 1):
                    k = t - 4
                    if 0 <= k < L.n:
                        dve.wait_ge(m2_done, done + k + 1 + i * step)
                        n = L.groups[k][2] * PAIR
                        if L.shrink:
                            dve.tensor_scalar(clamp[:, 0:2 * n], ps[:, M2_BANK, 0:2 * n], LAMBDA, -LAMBDA,
                                              ALU.min, ALU.max).then_inc(clamped, 1)
                            dve.wait_ge(clamped, shrunk + k + 1 + i * step)
                        for half in range(2):
                            rows = slice(half * SIDE, (half + 1) * SIDE)
                            for ri in range(2):
                                at = slice(ri * n, (ri + 1) * n)
                                to = u[ri * SIDE:(ri + 1) * SIDE, k % 2, half, 0:n]
                                if L.shrink:
                                    ins = dve.tensor_tensor(to, ps[rows, M2_BANK, at], clamp[rows, at], ALU.subtract)
                                else:
                                    ins = dve.tensor_copy(to, ps[rows, M2_BANK, at])
                        ins.then_inc(u_ready, 1)
                    k = t - 2
                    if 0 <= k < L.n and L.split:
                        dve.wait_ge(zf_ready, done + k + 1 + i * step)
                        width = L.groups[k][2] * P
                        dve.tensor_tensor(zfl[0:PAIR, k % 2, :, 0:width],
                                          ps[0:PAIR, T2_BANK, :].rearrange("p (n m) -> p n m", n=2)[:, :, 0:width],
                                          zfh[0:PAIR, k % 2, :, 0:width], ALU.subtract).then_inc(zf_low, 1)
                    k = t - 1
                    if 0 <= k < L.n:
                        dve.wait_ge(f2_done, done + k + 1 + i * step)
                        n = L.groups[k][2] * 2 * PAIR
                        dve.tensor_scalar(zs[:, k % 2, 0:n], ps[:, F2_BANK, 0:n],
                                          L.forward, None, ALU.mult).then_inc(zs_ready, 1)
                    if before and t < len(POST_BESIDE):
                        for p in POST_BESIDE[t][0] + POST_BESIDE[t][1]:
                            post(*before, p)
                    if before and before[0].index == 0:
                        if urgent:
                            start = AGGREGATE_AT[L.index] - CHUNKS // 2 + 1
                            chunks = range(2 * (t - start), 2 * (t - start) + 2)
                        else:
                            chunks = range(t - 3, t - 2)
                        for k in chunks:
                            if 0 <= k < CHUNKS:
                                unit_statistics(*before[1:], k)
                    beside(L, b, i, last, t)

            def beside(L, b, i, last, t):
                if L.index == 0 and first_of(i) and t in SPLIT_STEPS:
                    split(b * WPARTS + SPLIT_STEPS[t])
                if L.norm:
                    unit = (1, i) if b == 0 else None if last else (0, i + 1)
                else:
                    unit = (0, 0) if L.index == 0 and last and b == 1 else None
                if unit:
                    if first_of(unit[1]) and t == AGGREGATE_AT[L.index]:
                        aggregate(unit[0])
                    n = t - (L.n - 1)
                    if 0 <= n < CHUNKS // 2:
                        centre(*unit, 2 * n)
                        centre(*unit, 2 * n + 1)
                elif L.norm:
                    if t == L.n - 1:
                        statistics(0, 0)
                    if t == L.n + 1:
                        normalise(0, 0)

            def split(n):
                dve.wait_ge(wpart_high, n + 1)
                dve.tensor_tensor(wpart(w1l, w2l, n), wraw[:, :], wpart(w1h, w2h, n),
                                  ALU.subtract).then_inc(wpart_low, 1)

            def aggregate(b):
                dve.wait_ge(st_done, (2 * PAIRS - 1 + b) * ROWPAIRS)
                for r in range(b * ROWPAIRS, (b + 1) * ROWPAIRS):
                    dve.bn_aggr(mv[:, r, :], st[:, r].rearrange("p a b -> p (a b)")).then_inc(mv_ready, 1)

            def centre(b, i, k):
                if k % PART_CHUNKS == 0:
                    part = k // PART_CHUNKS
                    dve.wait_ge(x_loaded[b][part], 16 * (PAIRS + 1) + i * 16)
                    dve.wait_ge(stored[b][part], 16 * PAIRS + i * 16)
                if k == 0:
                    if first_of(i):
                        dve.wait_ge(mv_ready, (b + 1) * ROWPAIRS)
                        dve.wait_ge(rstd_ready, b + 1)
                for r in range(k * CHUNK, (k + 1) * CHUNK):
                    at, row = slice(r * PAIR, (r + 1) * PAIR), b * ROWPAIRS + r
                    ins = dve.tensor_scalar(res[:, b, at], xs[b][:, at], mv[:, row, 0:1], rstd[:, row:row + 1],
                                            ALU.subtract, ALU.mult)
                ins.then_inc(centred, 1)

            def post(L, b, i, t):
                base = CHUNKS * (L.units + b)
                k = t - POST_SKEW
                if k == 0:
                    if L.norm:
                        dve.wait_ge(sum_ready, b + 1 + i * 2)
                    else:
                        for part in range(PARTS):
                            dve.wait_ge(x_loaded[b][part], 16 * (PAIRS * L.index + 1) + i * 16)
                    if not L.norm and not (L.index == 0 and first_of(i)):
                        for part in range(PARTS):
                            dve.wait_ge(stored[b][part], 16 * PAIRS * L.index + i * 16)
                if k >= 0:
                    dve.wait_ge(f6_done, base + k + 1 + i * (2 * CHUNKS))
                    at = slice(k * CHUNK * PAIR, (k + 1) * CHUNK * PAIR)
                    dve.tensor_tensor(res[:, b, at], ps[:, F6_BANKS[k % 2], 0:CHUNK * PAIR], xs[b][:, at],
                                      ALU.add).then_inc(res_ready, 1)
                if t < CHUNKS:
                    dve.wait_ge(vt_high, base + t + 1 + i * (2 * CHUNKS))
                    dve.tensor_tensor(vtl[:, t % 2, :], ps[:, TT_BANKS[t], 0:CHUNK * PAIR], vth[:, t % 2, :],
                                      ALU.subtract).then_inc(vt_low, 1)

            def unit_statistics(b, i, k):
                dve.wait_ge(res_ready, CHUNKS * b + k + 1 + i * (2 * CHUNKS))
                for r in range(k * CHUNK, (k + 1) * CHUNK):
                    dve.bn_stats(st[:, b * ROWPAIRS + r, i if isinstance(i, int) else bass.ds(i, 1), :],
                                 res[:, b, r * PAIR:(r + 1) * PAIR]).then_inc(st_done, 1)

            def statistics(r, i):
                dve.wait_ge(m_loaded[r], 16 + i * 16)
                for j in range(4):
                    dve.bn_stats(stat[:, j, :], xm[:, r, j, :]).then_inc(st2_done, 1)
                dve.wait_ge(st2_done, 4 * (r + 1) + i * 8)
                dve.tensor_copy(counts[:, :], stat[:, :, 0])
                for j in range(4):
                    dve.bn_aggr(mv2[:, r, j, :], stat[:, j, :]).then_inc(mv2_ready, 1)

            def normalise(r, i):
                dve.wait_ge(mv2_ready, 4 * (r + 1) + i * 8)
                dve.wait_ge(rstd2_ready, r + 1 + i * 2)
                for j in range(4):
                    dve.tensor_scalar(xh[:, r, j, :], xm[:, r, j, :], mv2[:, r, j, 0:1], rstd2[:, r, j:j + 1],
                                      ALU.subtract, ALU.mult).then_inc(xh_ready, 1)

            def split_input(r, i, k):
                dve.wait_ge(mt_ready, KC * r + k + 1 + i * (2 * KC))
                dve.tensor_copy(mth[:, r, k, :], mt[:, k, :]).then_inc(mt_high, 1)
                dve.wait_ge(mt_high, KC * r + k + 1 + i * (2 * KC))
                dve.tensor_tensor(mtl[:, r, k, :], mt[:, k, :], mth[:, r, k, :],
                                  ALU.subtract).then_inc(mt_low, 1)

            def spectral_layer(L, previous, following):
                def body(i, last):
                    before = (previous, 1, PAIRS - 1) if first_of(i) else (L, 1, i - 1)
                    chain(L, 0, i, before if before[0] else None, last)
                    chain(L, 1, i, (L, 0, i), last)

                iterate(dve, PAIRS, body)
                if not following:
                    for t in range(POST_STEPS):
                        post(L, 1, PAIRS - 1, t)
                        if L.norm and t < KC:
                            split_input(0, 0, t)

            def token_mlp():
                def split_hidden(r, i, n):
                    dve.wait_ge(g_high, HC * r + n + 1 + i * (2 * HC))
                    dve.tensor_tensor(gl[:, n % 4, :], g[:, n % 2, :], gh[:, n % 4, :],
                                      ALU.subtract).then_inc(g_low, 1)

                def results(r, i):
                    if r == 0 and first_of(i):
                        for part in range(PARTS):
                            dve.wait_ge(stored[1][part], 16 * PAIRS * 2)
                    dve.wait_ge(skip_ready, r + 1 + i * 2)
                    wait_past(dve, m_stored[r], i * 16)
                    for j in range(4):
                        dve.wait_ge(mm2_done, 4 * r + j + 1 + i * 8)
                        dve.tensor_tensor(om[:, r, j, :], ps[:, MM2_BANKS[j], 0:CHANNELS], xm[:, r, j, :],
                                          ALU.add).then_inc(om_ready, 1)

                def tile(r, i, following):
                    for t in range(HC):
                        split_hidden(r, i, t)
                        if following:
                            if t == TURN_AT - 5:
                                statistics(*following)
                            if t == TURN_AT - 3:
                                normalise(*following)
                            if 0 <= t - TURN_AT < KC:
                                split_input(*following, t - TURN_AT)
                    results(r, i)

                def body(i, last):
                    tile(0, i, (1, i))
                    tile(1, i, None if last else (0, i + 1))

                iterate(dve, TILES // 2, body)

            spectral_layer(layers[0], None, layers[1])
            spectral_layer(layers[1], layers[0], None)
            token_mlp()
            spectral_layer(layers[2], None, layers[3])
            spectral_layer(layers[3], layers[2], None)

        @block.gpsimd
        def _(pool):
            pool.memset(power[:, :], -0.5).then_inc(rs_step, 1)
            pool.memset(eps[:, :], LN_EPS).then_inc(rs_step, 1)
            pool.wait_ge(s_const, 16)

            def weights(L, i):
                pool.wait_ge(w_loaded, 16 * (PAIRS * L.index + 1) + i * 16)
                wait_past(pool, m2_done, L.chain + i * (2 * L.n))
                real = C_SIGN + (1 if L.act == ACT.Gelu else 0)
                imag = SECOND + BLOCK
                src, to = wstage[0:ROWS], w[0:ROWS]
                pool.tensor_tensor(to[:, :, 0:BLOCK], src[:, :, 0:BLOCK],
                                   const[0:ROWS, C_SIGN:C_SIGN + 1].unsqueeze(1).to_broadcast([ROWS, 2, BLOCK]),
                                   ALU.mult).then_inc(w_ready, 1)
                pool.tensor_copy(to[:, :, BLOCK:ROWS], src[:, :, BLOCK:ROWS]).then_inc(w_ready, 1)
                pool.tensor_scalar(to[:, :, SECOND:imag], src[:, :, SECOND:imag], const[0:ROWS, real:real + 1], None,
                                   ALU.mult).then_inc(w_ready, 1)
                if L.act == ACT.Gelu:
                    pool.tensor_scalar(to[:, :, imag:BIAS], src[:, :, imag:BIAS],
                                       const[0:ROWS, C_SIGN + 2:C_SIGN + 3], None, ALU.mult).then_inc(w_ready, 1)
                else:
                    pool.tensor_copy(to[:, :, imag:BIAS], src[:, :, imag:BIAS]).then_inc(w_ready, 1)
                pool.tensor_copy(to[:, :, BIAS:], src[:, :, BIAS:]).then_inc(w_ready, 1)
                high = wh[0:PAIR]
                pool.tensor_tensor(high[:, :, 0:BLOCK], src[0:PAIR, :, 0:BLOCK],
                                   const[0:PAIR, C_SIGN:C_SIGN + 1].unsqueeze(1).to_broadcast([PAIR, 2, BLOCK]),
                                   ALU.mult).then_inc(w_ready, 1)
                pool.tensor_copy(high[:, :, BLOCK:ROWS], src[0:PAIR, :, BLOCK:ROWS]).then_inc(w_ready, 1)
                pool.wait_ge(w_ready, W_STEPS * (PAIRS * L.index + 1) - 1 + i * W_STEPS)
                pool.tensor_tensor(wl[0:PAIR], to[0:PAIR, :, 0:ROWS], high, ALU.subtract).then_inc(w_ready, 1)

            def norm_columns(i):
                if not first_of(i):
                    pool.wait_ge(shifted, i * 2)
                pool.tensor_tensor(gcol[0:PAIR, :], lncol[0:PAIR, bass.ds(i, 1), :].rearrange("p o a -> p (o a)"),
                                   const[0:PAIR, C_SIGN + 3:C_SIGN + 5], ALU.mult).then_inc(gcol_ready, 1)

            def gain(b, i):
                rv = res[:, b, :].rearrange("p (r c) -> p r c", c=PAIR)
                gain = lnrow[:, 0:1, bass.ds(i * PAIR, PAIR)].to_broadcast([P, ROWPAIRS, PAIR])
                pool.wait_ge(f1_done, CHUNKS * (layers[1].units + b + 1) + i * (2 * CHUNKS))
                pool.tensor_tensor(rv, rv, gain, ALU.mult).then_inc(gained, 1)

            def residual(b, i):
                xv = xs[b][:, :].rearrange("p (r c) -> p r c", c=PAIR)
                rv = res[:, b, :].rearrange("p (r c) -> p r c", c=PAIR)
                shift = lnrow[:, 1:2, bass.ds(i * PAIR, PAIR)].to_broadcast([P, ROWPAIRS, PAIR])
                pool.wait_ge(gained, b + 1 + i * 2)
                pool.tensor_tensor(xv, xv, rv, ALU.add).then_inc(ln_step, 1)
                pool.wait_ge(ln_step, b + 1 + i * 2)
                pool.tensor_tensor(xv, xv, shift, ALU.add).then_inc(sum_ready, 1)

            def spectral_layer(L, previous, following):
                def body(i, last):
                    if L.norm:
                        gain(1, i)
                        residual(1, i)
                    if not last:
                        if L.norm:
                            norm_columns(i + 1)
                        weights(L, i + 1)
                        if L.norm:
                            gain(0, i + 1)
                            residual(0, i + 1)
                    elif following:
                        if following.norm:
                            pool.wait_ge(s_wts, 48)
                            norm_columns(0)
                            root(0)
                        weights(following, 0)
                        if following.norm:
                            gain(0, 0)
                            root(1)
                            residual(0, 0)

                if not previous:
                    weights(L, 0)
                iterate(pool, PAIRS, body)

            def root(b):
                at = slice(b * ROWPAIRS, (b + 1) * ROWPAIRS)
                pool.wait_ge(mv_ready, (b + 1) * ROWPAIRS)
                pool.tensor_tensor(rstd[:, at], mv[:, at, 1], eps[:, :].to_broadcast([P, ROWPAIRS]), ALU.add).then_inc(rs_step, 1)
                pool.wait_ge(rs_step, 3 + b)
                pool.tensor_tensor(rstd[:, at], rstd[:, at], power[:, :].to_broadcast([P, ROWPAIRS]), ALU.pow).then_inc(rstd_ready, 1)

            def token_mlp():
                def root2(r, i):
                    pool.wait_ge(mv2_ready, 4 * (r + 1) + i * 8)
                    pool.tensor_tensor(rstd2[:, r, :], mv2[:, r, :, 1], eps[:, :].to_broadcast([P, 4]), ALU.add).then_inc(rs2_step, 1)
                    pool.wait_ge(rs2_step, r + 1 + i * 2)
                    pool.tensor_tensor(rstd2[:, r, :], rstd2[:, r, :], power[:, :].to_broadcast([P, 4]), ALU.pow).then_inc(rstd2_ready, 1)
                    pool.wait_ge(s_wts, 64)
                    pool.wait_ge(xh_ready, 4 * (r + 1) + i * 8)
                    pool.tensor_tensor(xm[:, r], xm[:, r], b2row[:, :].unsqueeze(1).to_broadcast([P, 4, CHANNELS]),
                                       ALU.add).then_inc(skip_ready, 1)

                with pool.Fori(0, TILES // 2) as i:
                    root2(0, i)
                    root2(1, i)

            spectral_layer(layers[0], None, layers[1])
            spectral_layer(layers[1], layers[0], None)
            token_mlp()
            spectral_layer(layers[2], None, layers[3])
            spectral_layer(layers[3], layers[2], None)


def host_constants():
    import numpy as np
    n, f = np.arange(SIDE), 2 * np.pi / SIDE
    half = np.arange(HALF)
    col = np.stack([np.cos(f * np.outer(n, half)), -np.sin(f * np.outer(n, half))], 1)
    col[:, 1, 0] = (-1.0) ** n
    d1 = np.kron(np.eye(2), col.reshape(SIDE, SIDE))
    inv = 2 * col.transpose(1, 2, 0)
    inv[:, 0] /= 2
    d6 = np.kron(np.eye(2), inv.reshape(SIDE, SIDE))
    c, s = np.cos(f * np.outer(n, n)), np.sin(f * np.outer(n, n))
    o = np.zeros((SIDE, SIDE))
    d2 = np.block([[c, -s], [s, c]])
    d2a, d2b = np.block([[c, -s], [o, o]]), np.block([[o, o], [c, -s]])
    d5 = np.block([[c, s], [-s, c]])
    d5a = np.block([[c, o], [-s, o]])

    def pair(first):
        m = np.zeros((2, 2, HALF, 2, 2 * SIDE))
        for slot, d in enumerate((first, d5)):
            m[:, slot, :, slot, :] = d.reshape(2, SIDE, 2 * SIDE)[:, :HALF]
        return m.reshape(P, 4 * SIDE)

    sign = np.ones((P, 5))
    sign[BLOCK:PAIR, 0:2] = -1
    sign[ONE_ROW, 1:3] = 1 / ONE_GELU
    sign[:, 4] = SIDE
    return np.concatenate([d1, np.eye(P), d2, d2a, d2b, d5, d6, pair(d5), pair(d5a), sign],
                          1).astype(np.float32)


def pack_spectral(w1, b1, w2, b2, one):
    import numpy as np
    t = np.zeros((BLOCKS, ROWS, W_COLS), np.float32)
    for row in range(2):
        rows = slice(row * BLOCK, (row + 1) * BLOCK)
        for to in range(2):
            t[:, rows, to * BLOCK:(to + 1) * BLOCK] = w1[row ^ to]
            t[:, rows, SECOND + to * BLOCK:SECOND + (to + 1) * BLOCK] = w2[row ^ to]
        t[:, ONE_ROW, SECOND + row * BLOCK:SECOND + (row + 1) * BLOCK] = b2[row]
        t[:, rows, BIAS] = b1[row]
    t[:, ONE_ROW, BIAS] = one
    return t


def kernel(**inputs):
    import numpy as np
    import concourse.bacc as bacc
    from concourse.bass_utils import run_bass_kernel_spmd

    a = {k: np.asarray(t) for k, t in inputs.items()}

    def all_blocks(t):
        return np.broadcast_to(t, (BLOCKS,) + t.shape)

    spectral = np.stack([
        pack_spectral(a["L0_conv_w1"], a["L0_conv_b1"], a["L0_conv_w2"], a["L0_conv_b2"], 1.0),
        pack_spectral(a["L1_conv_w1"], a["L1_conv_b1"], a["L1_conv_w2"], a["L1_conv_b2"], ONE_GELU),
        pack_spectral([all_blocks(a["L2_conv_w1r"].T), all_blocks(a["L2_conv_w1i"].T)],
                      [all_blocks(a["L2_conv_b1"][:, n]) for n in range(2)],
                      [all_blocks(a["L2_conv_w2r"].T), all_blocks(a["L2_conv_w2i"].T)],
                      [all_blocks(a["L2_conv_b2"][:, n]) for n in range(2)], 1.0),
        pack_spectral([a["L3_conv_w1"][..., n] for n in range(2)], [a["L3_conv_b1"][..., n] for n in range(2)],
                      [a["L3_conv_w2"][..., n] for n in range(2)], [a["L3_conv_b2"][..., n] for n in range(2)], 1.0)])
    arrays = {
        "x": a["x"].reshape(BATCH, SIDE * SIDE, CHANNELS),
        "consts": host_constants(),
        "spectral": spectral,
        "ln1": np.stack([a["L1_conv_ln1_g"], a["L1_conv_ln1_b"]]),
        "lncol": np.stack([a["L1_conv_ln1_g"], a["L1_conv_ln1_b"]], 1).reshape(PAIRS, PAIR, 2).transpose(1, 0, 2),
        "cols": np.concatenate([a["L1_conv_mlp_b1"].reshape(HC, P), a["L1_conv_ln2_g"].reshape(KC, P),
                                a["L1_conv_ln2_b"].reshape(KC, P)]).T,
        "w1": a["L1_conv_mlp_w1"],
        "w2": a["L1_conv_mlp_w2"],
        "b2": a["L1_conv_mlp_b2"],
    }
    arrays = {f"in_{k}": np.ascontiguousarray(t) for k, t in arrays.items()}
    nc = bacc.Bacc("TRN2", target_bir_lowering=False, num_devices=1)
    args = [nc.dram_tensor(k, t.shape, mybir.dt.from_np(t.dtype), kind="ExternalInput").ap() for k, t in arrays.items()]
    out = nc.dram_tensor("out", (BATCH, SIDE * SIDE, CHANNELS), F32, kind="ExternalOutput").ap()
    build(nc, *args, out)
    r = run_bass_kernel_spmd(nc, [arrays], core_ids=[0])
    return np.asarray(r.results[0]["out"]).reshape(BATCH, SIDE, SIDE, CHANNELS)
```
